# Optimizing a Trainium2 kernel written in Bass

```python
import numpy as np
import jax
import jax.numpy as jnp

def _softmax(x, axis=-1):
    return jax.nn.softmax(x, axis=axis)

def _gelu(x):
    return jax.nn.gelu(x, approximate=True)

def _silu(x):
    return jax.nn.silu(x)

def _sigmoid(x):
    return jax.nn.sigmoid(x)

def _layernorm(x, axis=-1, eps=1e-05):
    m = jnp.mean(x, axis=axis, keepdims=True)
    v = jnp.var(x, axis=axis, keepdims=True)
    return (x - m) / jnp.sqrt(v + eps)

def _scatter_add(tgt, idx, src, axis=0):
    return tgt.at[idx].add(src)

def _segment_sum(src, seg, n):
    return jax.ops.segment_sum(src, seg, n)
kernel_name = 'mk_gnn_preln_d2_gnn_r32_1e99b1'

def setup_inputs(seed: int=0):
    np.random.seed(seed)
    _w = jnp.asarray

    def _rec_inputs():
        import jax
        import jax.numpy as jnp
        _gk = jax.random.key(seed)
        x = -0.000202 + 1 * jax.random.normal(jax.random.fold_in(_gk, 1), (50000, 128), jnp.float32)
        src = jax.random.randint(jax.random.fold_in(_gk, 2), (25000,), 0, 50000, jnp.int32)
        dst = jax.random.randint(jax.random.fold_in(_gk, 3), (25000,), 0, 50000, jnp.int32)
        _o = jnp.argsort(dst, stable=True)
        src = src[_o]
        dst = dst[_o]
        return (x, src, dst)
    x, src, dst = _rec_inputs()

    def _L0_gnn_setup():
        import jax, jax.numpy as jnp
        import numpy as np
        N = 50000
        E = 25000
        D = 128
        MAX_NODES = 4
        EPS = 1e-05

        def sort_conv(x, edge_index, blank, W, b, cw, cb, a):
            n, d = x.shape
            e = edge_index.shape[1]
            src, dst = (edge_index[0], edge_index[1])
            msgs = x[src]
            order = jnp.argsort(dst)
            dst_s = dst[order]
            counts = jax.ops.segment_sum(jnp.ones((e,), jnp.int32), dst, num_segments=n + 1)
            starts = jnp.concatenate([jnp.zeros((1,), jnp.int32), jnp.cumsum(counts)[:-1].astype(jnp.int32)])
            pos = jnp.arange(e, dtype=jnp.int32) - starts[dst_s]
            slot = jnp.where(pos < MAX_NODES, pos, MAX_NODES)
            dense = jnp.zeros((n + 1, MAX_NODES + 1, d), x.dtype).at[dst_s, slot].set(msgs[order])
            mask = jnp.zeros((n + 1, MAX_NODES + 1), bool).at[dst_s, slot].set(True)
            dense, mask = (dense[:, :MAX_NODES], mask[:, :MAX_NODES])
            blank_p = W @ blank + b
            filled = dense + (~mask)[..., None].astype(x.dtype) * blank_p
            srt = jnp.sort(filled, axis=1)
            out = jnp.einsum('nmd,m->nd', srt, cw) + cb
            node_out, blank_new = (out[:-1], out[-1])
            return (a * x + node_out, a * blank + blank_new)

        def batch_norm(h, g, be):
            mu = h.mean(0)
            var = h.var(0)
            return (h - mu) / jnp.sqrt(var + EPS) * g + be
        key = jax.random.key(seed)
        ks = jax.random.split(key, 16)
        inp = {'x': jax.random.normal(ks[0], (N, D), jnp.float32), 'edge_index': jax.random.randint(ks[1], (2, E), 0, N, jnp.int32)}
        for i in range(2):
            o = 2 + 6 * i
            W = jax.random.normal(ks[o], (D, D), jnp.float32) * (2.0 / (D + D)) ** 0.5
            W = W / jnp.linalg.norm(W, axis=1, keepdims=True)
            inp[f'W{i}'] = W
            inp[f'b{i}'] = jnp.zeros((D,), jnp.float32)
            inp[f'cw{i}'] = jax.random.normal(ks[o + 1], (MAX_NODES,), jnp.float32) * (2.0 / (MAX_NODES + 1)) ** 0.5
            inp[f'cb{i}'] = jnp.zeros((1,), jnp.float32)
            inp[f'a{i}'] = jax.random.uniform(ks[o + 2], (1,), jnp.float32, -1.0, 1.0)
            inp[f'g{i}'] = jnp.ones((D,), jnp.float32)
            inp[f'be{i}'] = jnp.zeros((D,), jnp.float32)
            inp[f'blank{i}'] = jnp.zeros((D,), jnp.float32)
        return inp
    _L0_gnn_all = _L0_gnn_setup()
    _L0_gnn_in = {k: v for k, v in _L0_gnn_all.items() if k in ('W0', 'b0', 'cw0', 'cb0', 'a0', 'g0', 'be0', 'blank0', 'W1', 'b1', 'cw1', 'cb1', 'a1', 'g1', 'be1', 'blank1')}
    del _L0_gnn_all

    def _L1_gnn_setup():
        import jax, jax.numpy as jnp
        import numpy as np
        N_NODES = 3125
        N_EDGES = 18750
        H = 128
        NUM_STEPS = 5
        key = jax.random.key(seed)
        ks = jax.random.split(key, 8)
        s = 0.05
        return {'x': jax.random.normal(ks[0], (N_NODES, H), dtype=jnp.float32), 'edge_index': jax.random.randint(ks[1], (2, N_EDGES), 0, N_NODES, dtype=jnp.int64), 'W_msg': jax.random.normal(ks[2], (H, H), dtype=jnp.float32) * s, 'b_msg': jax.random.normal(ks[3], (H,), dtype=jnp.float32) * s, 'W_ih': jax.random.normal(ks[4], (3 * H, H), dtype=jnp.float32) * s, 'W_hh': jax.random.normal(ks[5], (3 * H, H), dtype=jnp.float32) * s, 'b_ih': jax.random.normal(ks[6], (3 * H,), dtype=jnp.float32) * s, 'b_hh': jax.random.normal(ks[7], (3 * H,), dtype=jnp.float32) * s}
    _L1_gnn_all = _L1_gnn_setup()
    _L1_gnn_in = {k: v for k, v in _L1_gnn_all.items() if k in ('W_msg', 'b_msg', 'W_ih', 'W_hh', 'b_ih', 'b_hh')}
    del _L1_gnn_all
    return {'x': x, 'src': src, 'dst': dst, 'L0_gnn_W0': _L0_gnn_in['W0'], 'L0_gnn_b0': _L0_gnn_in['b0'], 'L0_gnn_cw0': _L0_gnn_in['cw0'], 'L0_gnn_cb0': _L0_gnn_in['cb0'], 'L0_gnn_a0': _L0_gnn_in['a0'], 'L0_gnn_g0': _L0_gnn_in['g0'], 'L0_gnn_be0': _L0_gnn_in['be0'], 'L0_gnn_blank0': _L0_gnn_in['blank0'], 'L0_gnn_W1': _L0_gnn_in['W1'], 'L0_gnn_b1': _L0_gnn_in['b1'], 'L0_gnn_cw1': _L0_gnn_in['cw1'], 'L0_gnn_cb1': _L0_gnn_in['cb1'], 'L0_gnn_a1': _L0_gnn_in['a1'], 'L0_gnn_g1': _L0_gnn_in['g1'], 'L0_gnn_be1': _L0_gnn_in['be1'], 'L0_gnn_blank1': _L0_gnn_in['blank1'], 'L1_gnn_W_msg': _L1_gnn_in['W_msg'], 'L1_gnn_b_msg': _L1_gnn_in['b_msg'], 'L1_gnn_W_ih': _L1_gnn_in['W_ih'], 'L1_gnn_W_hh': _L1_gnn_in['W_hh'], 'L1_gnn_b_ih': _L1_gnn_in['b_ih'], 'L1_gnn_b_hh': _L1_gnn_in['b_hh']}

def reference(x, src, dst, L0_gnn_W0, L0_gnn_b0, L0_gnn_cw0, L0_gnn_cb0, L0_gnn_a0, L0_gnn_g0, L0_gnn_be0, L0_gnn_blank0, L0_gnn_W1, L0_gnn_b1, L0_gnn_cw1, L0_gnn_cb1, L0_gnn_a1, L0_gnn_g1, L0_gnn_be1, L0_gnn_blank1, L1_gnn_W_msg, L1_gnn_b_msg, L1_gnn_W_ih, L1_gnn_W_hh, L1_gnn_b_ih, L1_gnn_b_hh):
    import jax
    import jax.numpy as jnp

    def _L0_gnn_ref(x, edge_index, W0, b0, cw0, cb0, a0, g0, be0, blank0, W1, b1, cw1, cb1, a1, g1, be1, blank1):
        import jax, jax.numpy as jnp
        import numpy as np
        N = 50000
        E = 25000
        D = 128
        MAX_NODES = 4
        EPS = 1e-05

        def sort_conv(x, edge_index, blank, W, b, cw, cb, a):
            n, d = x.shape
            e = edge_index.shape[1]
            src, dst = (edge_index[0], edge_index[1])
            msgs = x[src]
            order = jnp.argsort(dst)
            dst_s = dst[order]
            counts = jax.ops.segment_sum(jnp.ones((e,), jnp.int32), dst, num_segments=n + 1)
            starts = jnp.concatenate([jnp.zeros((1,), jnp.int32), jnp.cumsum(counts)[:-1].astype(jnp.int32)])
            pos = jnp.arange(e, dtype=jnp.int32) - starts[dst_s]
            slot = jnp.where(pos < MAX_NODES, pos, MAX_NODES)
            dense = jnp.zeros((n + 1, MAX_NODES + 1, d), x.dtype).at[dst_s, slot].set(msgs[order])
            mask = jnp.zeros((n + 1, MAX_NODES + 1), bool).at[dst_s, slot].set(True)
            dense, mask = (dense[:, :MAX_NODES], mask[:, :MAX_NODES])
            blank_p = W @ blank + b
            filled = dense + (~mask)[..., None].astype(x.dtype) * blank_p
            srt = jnp.sort(filled, axis=1)
            out = jnp.einsum('nmd,m->nd', srt, cw) + cb
            node_out, blank_new = (out[:-1], out[-1])
            return (a * x + node_out, a * blank + blank_new)

        def batch_norm(h, g, be):
            mu = h.mean(0)
            var = h.var(0)
            return (h - mu) / jnp.sqrt(var + EPS) * g + be
        layers = [(W0, b0, cw0, cb0, a0, g0, be0, blank0), (W1, b1, cw1, cb1, a1, g1, be1, blank1)]
        for W, b, cw, cb, a, g, be, blank in layers:
            h, _ = sort_conv(x, edge_index, blank, W, b, cw, cb, a)
            h = batch_norm(h, g, be)
            x = x + h
        return x

    def _L1_gnn_ref(x, edge_index, W_msg, b_msg, W_ih, W_hh, b_ih, b_hh):
        import jax, jax.numpy as jnp
        import numpy as np
        N_NODES = 3125
        N_EDGES = 18750
        H = 128
        NUM_STEPS = 5
        num_nodes = x.shape[0]
        row, col = (edge_index[0], edge_index[1])

        def step(h, _):
            messages = h[col] @ W_msg.T + b_msg
            agg = jax.ops.segment_sum(messages, row, num_segments=num_nodes)
            gi = agg @ W_ih.T + b_ih
            gh = h @ W_hh.T + b_hh
            i_r, i_z, i_n = jnp.split(gi, 3, axis=-1)
            h_r, h_z, h_n = jnp.split(gh, 3, axis=-1)
            r = jax.nn.sigmoid(i_r + h_r)
            z = jax.nn.sigmoid(i_z + h_z)
            n = jnp.tanh(i_n + r * h_n)
            h_new = (1.0 - z) * n + z * h
            return (h_new, None)
        h, _ = jax.lax.scan(step, x, None, length=NUM_STEPS)
        return h
    edge_index = jnp.stack([src, dst])
    h = jnp.maximum(_layernorm(x, axis=-1), 0.0)
    x = x + _L0_gnn_ref(h, edge_index, L0_gnn_W0, L0_gnn_b0, L0_gnn_cw0, L0_gnn_cb0, L0_gnn_a0, L0_gnn_g0, L0_gnn_be0, L0_gnn_blank0, L0_gnn_W1, L0_gnn_b1, L0_gnn_cw1, L0_gnn_cb1, L0_gnn_a1, L0_gnn_g1, L0_gnn_be1, L0_gnn_blank1)
    h = jnp.maximum(_layernorm(x, axis=-1), 0.0)
    x = x + _L1_gnn_ref(h, edge_index, L1_gnn_W_msg, L1_gnn_b_msg, L1_gnn_W_ih, L1_gnn_W_hh, L1_gnn_b_ih, L1_gnn_b_hh)
    return x

_drawn_inputs = setup_inputs


def setup_inputs(seed=0):
    import zlib

    import numpy as np

    out = dict(_drawn_inputs(seed))
    spreads = {'L0_gnn_b0': (0.0, 0.1),
     'L0_gnn_g0': (1.0, 0.2),
     'L0_gnn_be0': (0.0, 0.1),
     'L0_gnn_blank0': (0.0, 0.1),
     'L0_gnn_b1': (0.0, 0.1),
     'L0_gnn_g1': (1.0, 0.2),
     'L0_gnn_be1': (0.0, 0.1),
     'L0_gnn_blank1': (0.0, 0.1)}
    factors = {'L1_gnn_b_msg': 3.252, 'L1_gnn_b_hh': 3.179}
    for name, (base, spread) in spreads.items():
        noise = np.random.default_rng([zlib.crc32(name.encode()), seed]).standard_normal(out[name].shape)
        drawn = base * np.exp(spread * noise) if base else spread * noise
        out[name] = jnp.asarray(drawn.astype(out[name].dtype))
    for name, factor in factors.items():
        out[name] = (out[name] * factor).astype(out[name].dtype)
    return out
```

```python
from contextlib import ExitStack

import concourse.bass as bass
from concourse import mybir

F32 = mybir.dt.float32
BF16 = mybir.dt.bfloat16
I32 = mybir.dt.int32
ALU = mybir.AluOpType
ACT = mybir.ActivationFunctionType
AX = mybir.AxisListType

P = 128
N, D, E = 50000, 128, 25000
LO, HI = 128, 392
NPAD = LO * HI
EC = 196
EPAD = P * EC
EREM = E - (P - 1) * EC
RT = 8
NCH = NPAD // (P * RT)
LASTP = (N - (NCH - 1) * P * RT) // RT
EQ = EC // NCH
JG = 14
NG = EC // JG
CW = 512
NACT = EPAD // CW
SW = P + 1
IDW = D + 4
LNEPS = 1e-5
BNEPS = 1e-5
STEPS = 5
FAR = 1 << 20


class Steps:

    def __init__(self, eng, sem):
        self.eng, self.sem, self.base, self.n = eng, sem, 0, 0

    def mark(self, ins):
        ins.then_inc(self.sem, 1)
        self.n += 1

    def here(self):
        return self.base + self.n

    def wait(self):
        self.eng.wait_ge(self.sem, self.here())


def engine_loop(eng, trips, body, steps=None, per=0):
    if steps is None:
        with eng.Fori(0, trips) as k:
            body(k)
        return
    base, n = steps.base, steps.n
    with eng.Fori(0, trips) as k:
        steps.base, steps.n = base + n + k * per, 0
        body(k)
        assert steps.n == per, (steps.n, per)
    steps.base, steps.n = base, n + trips * per


def chunk_loop(eng, body, n=NCH, steps=None, per=0, peel=2):
    for i in range(peel):
        body(i, i % 2, i // 2)

    def both(k):
        body(2 * k + peel, 0, k + peel // 2)
        body(2 * k + peel + 1, 1, k + peel // 2)

    engine_loop(eng, (n - peel) // 2, both, steps, 2 * per)
    if n % 2:
        body(n - 1, 0, n // 2)


def two_halves(eng, first, second, half=EPAD // CW, tail=0):
    for c in range(3):
        first(c, c % 2, c // 2)

    def a(k):
        first(2 * k + 3, 1, k + 1)
        first(2 * k + 4, 0, k + 2)

    engine_loop(eng, half // 2 - 1, a)
    second(half, 1, half // 2)

    def b(k):
        second(2 * k + half + 1, 0, k + (half + 1) // 2)
        second(2 * k + half + 2, 1, k + (half + 1) // 2)

    engine_loop(eng, (half - tail) // 2, b)
    for c in range(2 * half - tail, 2 * half):
        second(c, c % 2, c // 2)


def behind(par, use, lag):
    return (par - lag) % 2, use - (lag + 1 - par) // 2


def need(eng, sem, value):
    if not (isinstance(value, int) and value <= 0):
        eng.wait_ge(sem, value)


def build(nc, x, src, dst, conv, gru, out):
    ctx = ExitStack()

    def sb(name, shape, dt=F32, c=ctx):
        return c.enter_context(nc.sbuf_tensor(name, shape, dt))

    def pb(name, shape, dt=F32, c=ctx):
        return c.enter_context(nc.psum_tensor(name, shape, dt))

    def sem(name):
        return ctx.enter_context(nc.semaphore(name))

    def dram(name, shape, dt=F32):
        return nc.dram_tensor(name, shape, dt).ap()

    h_tab = [dram("h0_tab", (NPAD, D)), dram("h1_tab", (NPAD, D))]
    o_tab = [dram("o0_tab", (NPAD, D)), dram("o1_tab", (NPAD, D))]
    x2_tab = dram("x2_tab", (NPAD, IDW))
    ht_tab = dram("ht_tab", (D, NPAD))
    msg_tab = [dram("msg0_tab", (NPAD, D)), dram("msg1_tab", (NPAD, D))]
    node_tab = dram("node_tab", (NPAD, 2), I32)
    sort_tab = dram("sort_tab", (EPAD, 2), I32)

    with ctx:
        ident = sb("ident", [P, P])
        identb = sb("identb", [P, P], BF16)
        ones = sb("ones", [P, P])
        ones_last = sb("ones_last", [P, P])
        later = sb("later", [P, P])
        row0 = sb("row0", [P, P])
        iota_p = sb("iota_p", [P, 1])
        iota_w = sb("iota_w", [P, HI])
        epsc = sb("epsc", [P, 1])
        edge_src = sb("edge_src", [P, EC + 3], I32)
        gat_src = sb("gat_src", [P, EC + 3], I32)
        edge_dst = sb("edge_dst", [P, EC + 4], I32)
        same1 = sb("same1", [P, EC + 2], I32)
        same2 = sb("same2", [P, EC], I32)
        put_idx = sb("put_idx", [P, EC], I32)
        src_at = sb("src_at", [P, EC], I32)
        dst_at = sb("dst_at", [P, EC], I32)
        occ = sb("occ", [P, EC])
        look = sb("look", [P, EC, 2], I32)
        pair = sb("pair", [P, EC, 2], I32)
        sort_at = sb("sort_at", [P, EC], I32)
        node_pos = sb("node_pos", [P, HI], I32)

        s_ld = sem("s1_load")
        s_ms = sem("s1_memset")
        s_io = sem("s1_iota")
        s_dv = sem("s1_dve")
        s_pe = sem("s1_pe")
        blank_o = [sb("blank_o0", [P, D]), sb("blank_o1", [P, D])]
        blank_p = [sb("blank_p0", [P, D]), sb("blank_p1", [P, D])]
        cwb = [sb(f"cwb{i}", [P, 4]) for i in range(2)]
        cbb = [sb(f"cbb{i}", [P, 1]) for i in range(2)]
        ab = [sb(f"ab{i}", [P, 1]) for i in range(2)]
        gb = [sb(f"gb{i}", [P, D]) for i in range(2)]
        beb = [sb(f"beb{i}", [P, D]) for i in range(2)]
        filled = [sb("o_blank0", [P, RT * D]), sb("o_blank1", [P, RT * D])]
        c1 = ExitStack()
        with c1:
            iw_i = sb("iw_i", [P, HI], I32, c1)
            ip_i = sb("ip_i", [P, 1], I32, c1)
            wt = [sb(f"wt{i}", [P, D], F32, c1) for i in range(2)]
            bb = [sb(f"bb{i}", [P, D], F32, c1) for i in range(2)]
            blc = [sb(f"blc{i}", [P, 1], F32, c1) for i in range(2)]
            blw = [sb(f"blw{i}", [P, P], F32, c1) for i in range(2)]
            dstf = sb("dstf", [P, EC + 4], F32, c1)
            tmpf = sb("tmpf", [P, EC], F32, c1)
            tmpg = sb("tmpg", [P, EC], F32, c1)
            pbl = [pb(f"pbl{i}", [P, D], F32, c1) for i in range(2)]
            block = c1.enter_context(nc.Block())
            loads = []

            @block.sync
            def _(sp):
                sp.wait_ge(s_ms, 2)
                m = (P - 1) * EC
                for t, s, o in ((edge_src, src, 0), (edge_dst, dst, 1)):
                    loads.append(sp.dma_start(t[0:P - 1, o:o + EC], s[0:m].rearrange("(p j) -> p j", j=EC)))
                    loads.append(sp.dma_start(t[P - 1:P, o:o + EREM], s[m:E].rearrange("(p j) -> p j", p=1)))
                    loads.append(sp.dma_start(t[0:P - 2, o + EC:o + EC + 3],
                                              s[EC:m].rearrange("(p j) -> p j", j=EC)[:, 0:3]))
                    loads.append(sp.dma_start(t[P - 2:P - 1, o + EC:o + EC + 3],
                                              s[m:m + 3].rearrange("(p j) -> p j", p=1)))
                loads.append(sp.dma_start(edge_dst[1:P, 0:1], dst[0:m].rearrange("(p j) -> p j", j=EC)[:, EC - 1:EC],
                                          allow_slow_non_contiguous=True))
                for i in range(2):
                    W, b, cw, cb, a, g, be, bl = conv[i]
                    loads.append(sp.dma_start(wt[i][:], W))
                    loads.append(sp.dma_start(blc[i][:], bl.rearrange("(p o) -> p o", o=1)))
                    for t, v in ((bb[i], b), (cwb[i], cw), (cbb[i], cb), (ab[i], a), (gb[i], g), (beb[i], be)):
                        loads.append(sp.dma_start(t[:], v.partition_broadcast(P)))
                for ins in loads:
                    ins.then_inc(s_ld, 16)

            NLOAD = 9 + 16

            @block.gpsimd
            def _(pool):
                nc.gpsimd.memset(edge_src[:], NPAD).then_inc(s_ms, 1)
                nc.gpsimd.memset(edge_dst[:], -1).then_inc(s_ms, 1)
                nc.gpsimd.iota(iw_i[:], [[1, HI]], base=0, channel_multiplier=0).then_inc(s_io, 1)
                nc.gpsimd.iota(ip_i[:], [[1, 1]], base=0, channel_multiplier=1).then_inc(s_io, 1)

            @block.vector
            def _(dve):
                st = Steps(dve, s_dv)
                dve.wait_ge(s_io, 2)
                st.mark(nc.vector.memset(ones[:], 1.0))
                st.mark(nc.vector.memset(epsc[:], LNEPS))
                st.mark(nc.vector.tensor_copy(iota_w[:], iw_i[:]))
                st.mark(nc.vector.tensor_copy(iota_p[:], ip_i[:]))
                st.wait()
                st.mark(nc.vector.tensor_scalar(ident[:], iota_w[:, 0:P], iota_p[:, 0:1], None, ALU.is_equal))
                st.mark(nc.vector.tensor_scalar(identb[:], iota_w[:, 0:P], iota_p[:, 0:1], None, ALU.is_equal))
                st.mark(nc.vector.tensor_scalar(later[:], iota_w[:, 0:P], iota_p[:, 0:1], None, ALU.is_gt))
                st.mark(nc.vector.tensor_scalar(row0[:], ones[:], iota_p[:, 0:1], 0.0, ALU.mult, ALU.is_equal))
                st.mark(nc.vector.tensor_scalar(ones_last[:], ones[:], iota_p[:, 0:1], float(LASTP),
                                                ALU.mult, ALU.is_lt))
                dve.wait_ge(s_ld, 16 * NLOAD)
                for i in range(2):
                    st.mark(nc.vector.tensor_scalar(blw[i][:], ones[:], blc[i][:, 0:1], None, ALU.mult))
                st.mark(nc.vector.tensor_copy(dstf[:], edge_dst[:]))
                for at, e in ((src_at, edge_src[:, 0:EC]), (dst_at, edge_dst[:, 1:EC + 1])):
                    st.wait()
                    st.mark(nc.vector.tensor_scalar(at[:], e, LO - 1, None, ALU.bitwise_and))
                    st.mark(nc.vector.tensor_scalar(sort_at[:], e, 7, None, ALU.logical_shift_right))
                    st.wait()
                    st.mark(nc.vector.tensor_copy(tmpf[:], at[:]))
                    st.mark(nc.vector.tensor_copy(tmpg[:], sort_at[:]))
                    st.wait()
                    st.mark(nc.vector.tensor_scalar(tmpf[:], tmpf[:], float(HI), None, ALU.mult))
                    st.wait()
                    st.mark(nc.vector.tensor_tensor(tmpf[:], tmpf[:], tmpg[:], ALU.add))
                    st.wait()
                    st.mark(nc.vector.tensor_scalar(at[:], tmpf[:], float(NPAD - 1), None, ALU.min))
                st.wait()
                st.mark(nc.vector.tensor_scalar(gat_src[:], edge_src[:], float(N), None, ALU.min))
                st.mark(nc.vector.tensor_tensor(same1[:], dstf[:, 1:EC + 3], dstf[:, 2:EC + 4], ALU.is_equal))
                st.mark(nc.vector.tensor_tensor(same2[:], dstf[:, 1:EC + 1], dstf[:, 3:EC + 3], ALU.is_equal))
                st.mark(nc.vector.tensor_tensor(tmpf[:], dstf[:, 1:EC + 1], dstf[:, 0:EC], ALU.is_equal))
                st.mark(nc.vector.tensor_scalar(tmpg[:], dstf[:, 1:EC + 1], 0.0, None, ALU.is_lt))
                st.wait()
                st.mark(nc.vector.tensor_tensor(tmpf[:], tmpf[:], tmpg[:], ALU.add))
                st.wait()
                st.mark(nc.vector.scalar_tensor_tensor(put_idx[:], tmpf[:], float(FAR), dstf[:, 1:EC + 1],
                                                       ALU.mult, ALU.add))
                dve.wait_ge(s_pe, 2)
                for i in range(2):
                    st.mark(nc.vector.tensor_tensor(blank_p[i][:], pbl[i][:], bb[i][:], ALU.add))
                st.wait()
                for i in range(2):
                    st.mark(nc.vector.tensor_scalar(blank_o[i][:], blank_p[i][:], cwb[i][:, 0:1], cbb[i][:, 0:1],
                                                    ALU.mult, ALU.add))
                for m in range(1, 4):
                    st.wait()
                    for i in range(2):
                        st.mark(nc.vector.scalar_tensor_tensor(blank_o[i][:], blank_p[i][:], cwb[i][:, m:m + 1],
                                                               blank_o[i][:], ALU.mult, ALU.add))
                st.wait()
                for i in range(2):
                    st.mark(nc.vector.tensor_copy(filled[i][:].rearrange("p (t f) -> p t f", f=D),
                                                  blank_o[i][:].unsqueeze(1).to_broadcast([P, RT, D])))
                st.wait()

            @block.tensor
            def _(pe):
                pe.wait_ge(s_dv, 11)
                for i in range(2):
                    nc.tensor.matmul(pbl[i][:], blw[i][:], wt[i][:], start=True, stop=True).then_inc(s_pe, 1)

        s_fill = sem("s2_fill")
        s_xin = [sem("s2_x0"), sem("s2_x1")]
        s_xfree = [sem("s2_xf0"), sem("s2_xf1")]
        s_pad = sem("s2_pad")
        s_stat = sem("s2_stat")
        s_root = sem("s2_root")
        s_cols = sem("s2_cols")
        s_rows = sem("s2_rows")
        s_hout = [sem("s2_h0"), sem("s2_h1")]
        s_dv2 = sem("s2_dve")
        s_tick = sem("s2_tick")
        s_all = sem("s2_allsrc")
        s_hot = sem("s2_hot")
        s_hotT = sem("s2_hotT")
        s_hotc = sem("s2_hotc")
        s_cnt = sem("s2_cnt")
        s_run = sem("s2_run")
        s_look = sem("s2_look")
        s_red = sem("s2_red")
        cnt_lo = sb("cnt_lo", [P, 2, HI])
        c2 = ExitStack()
        with c2:
            xb = [sb(f"xb{i}", [P, RT, D], F32, c2) for i in range(2)]
            hb = [sb(f"hb{i}", [P, RT, D], F32, c2) for i in range(2)]
            stats = sb("stats", [P, RT, 6], F32, c2)
            mv = sb("mv", [P, 2, RT, 2], F32, c2)
            root = sb("root", [P, 2, RT], F32, c2)
            cols = sb("ln_cols", [P, 2, 2, RT], F32, c2)
            allsrc = sb("allsrc", [P, EPAD], I32, c2)
            srcf = sb("srcf", [P, EC], F32, c2)
            lof = sb("lof", [P, EC], F32, c2)
            hif = sb("hif", [P, EC], F32, c2)
            tmpi = sb("tmpi", [P, EC], I32, c2)
            hot_lo = sb("hot_lo", [P, EQ, P], BF16, c2)
            hot_hi = sb("hot_hi", [P, 2, EQ, HI], BF16, c2)
            hotT = sb("hotT", [P, 2, P], F32, c2)
            earlier = sb("earlier", [P, P], F32, c2)
            within = sb("within", [P, EC], F32, c2)
            before = sb("before", [P, EC], F32, c2)
            sums = sb("sums", [P, 2, EQ], F32, c2)
            junk = sb("junk", [P, P], F32, c2)
            junk2 = sb("junk2", [P, HI], F32, c2)
            psT = pb("psT", [P, P], BF16, c2)
            psC = pb("psC", [P, HI], F32, c2)
            psL = [pb(f"psL{i}", [P, HI], F32, c2) for i in range(EQ)]
            block = c2.enter_context(nc.Block())
            DV = 2 * RT + 4 + 4 * EQ

            @block.sync
            def _(sp):
                sp.wait_ge(s_pad, 1)
                sp.dma_start(allsrc[:, 0:E], src.partition_broadcast(P)).then_inc(s_all, 16)
                xf = x[0:(NCH - 1) * P * RT, :].rearrange("(c p t) f -> c p t f", p=P, t=RT)
                of = [o_tab[i].rearrange("(c p t) f -> c p (t f)", p=P, t=RT) for i in range(2)]

                def load(i, par, use):
                    sp.wait_ge(s_xfree[par], use + 1)
                    sp.dma_start(xb[par][:], xf[bass.ds(i, 1)].rearrange("c p t f -> (c p) t f")
                                 ).then_inc(s_xin[par], 16)
                    for q in range(2):
                        sp.dma_start(of[q][bass.ds(i, 1)].rearrange("c p n -> (c p) n"), filled[q][:]
                                     ).then_inc(s_fill, 16)

                chunk_loop(sp, load, NCH - 1)
                sp.wait_ge(s_xfree[0], NCH // 2 + 1)
                sp.wait_ge(s_pad, 2)
                sp.dma_start(xb[0][0:LASTP], x[(NCH - 1) * P * RT:N, :].rearrange("(p t) f -> p t f", t=RT)
                             ).then_inc(s_xin[0], 16)
                for q in range(2):
                    sp.dma_start(of[q][NCH - 1], filled[q][:]).then_inc(s_fill, 16)
                sp.wait_ge(s_fill, 16 * 2 * NCH)

            @block.gpsimd
            def _(pool):
                nc.gpsimd.memset(allsrc[:, E:EPAD], NPAD).then_inc(s_pad, 1)
                pool.wait_ge(s_xfree[0], NCH // 2 + 1)
                nc.gpsimd.memset(xb[0][96:P], 0.0).then_inc(s_pad, 1)

            @block.vector
            def _(dve):
                st = Steps(dve, s_dv2)
                ev = allsrc[:, :].rearrange("p (q j) -> p q j", j=EC)
                st.mark(nc.vector.memset(cnt_lo[:, 0], 0.0))
                st.mark(nc.vector.tensor_copy(srcf[:], edge_src[:, 0:EC]))
                st.mark(nc.vector.tensor_scalar(tmpi[:], edge_src[:, 0:EC], LO - 1, None, ALU.bitwise_and))
                st.wait()
                st.mark(nc.vector.tensor_copy(lof[:], tmpi[:]))
                st.wait()
                st.mark(nc.vector.tensor_scalar(tmpi[:], edge_src[:, 0:EC], 7, None, ALU.logical_shift_right))
                st.wait()
                st.mark(nc.vector.tensor_copy(hif[:], tmpi[:]))
                st.mark(nc.vector.tensor_scalar(earlier[:], iota_w[:, 0:P], iota_p[:, 0:1], None, ALU.is_lt))
                st.wait()
                dve.sem_inc(s_run, 1)
                dve.sem_inc(s_red, EQ)
                dve.wait_ge(s_all, 16)

                def reduce(i, par):
                    for q in range(EQ):
                        dve.wait_ge(s_look, EQ * i + q + 1)
                        st.wait()
                        ins = nc.vector.tensor_tensor_reduce(
                            out=junk2[:], in0=psL[q][:], in1=hot_hi[:, par, q, :], scale=1.0, scalar=0.0,
                            op0=ALU.mult, op1=ALU.add, accum_out=sums[:, 0, q:q + 1])
                        st.mark(ins)
                        st.wait()
                        dve.sem_inc(s_red, 1)
                    st.mark(nc.vector.tensor_copy(before[:, bass.ds(EQ * i, EQ)], sums[:, 0, :]))

                def chunk(i, par, use):
                    first = isinstance(i, int) and i == 0
                    for q in range(EQ):
                        j = EQ * i + q
                        if not first:
                            dve.wait_ge(s_cnt, EQ * (i - 1) + q + 1)
                        st.mark(nc.vector.tensor_scalar(hot_lo[:, q, :], iota_w[:, 0:P], lof[:, bass.ds(j, 1)], None,
                                                        ALU.is_equal))
                        st.mark(nc.vector.tensor_scalar(hot_hi[:, par, q, :], iota_w[:], hif[:, bass.ds(j, 1)], None,
                                                        ALU.is_equal))
                        st.wait()
                        dve.sem_inc(s_hot, 1)
                        st.mark(nc.vector.scalar_tensor_tensor(
                            junk[:], ev[:, :, bass.ds(j, 1)].rearrange("p q j -> p (q j)"), srcf[:, bass.ds(j, 1)],
                            earlier[:], ALU.is_equal, ALU.mult, accum_out=sums[:, 1, q:q + 1]))
                    st.wait()
                    st.mark(nc.vector.tensor_copy(within[:, bass.ds(EQ * i, EQ)], sums[:, 1, :]))
                    dve.wait_ge(s_xin[par], 16 * (use + 1))
                    for t in range(RT):
                        st.mark(nc.vector.bn_stats(stats[:, t, :], xb[par][:, t, :]))
                    st.wait()
                    dve.sem_inc(s_tick, 1)
                    for t in range(RT):
                        st.mark(nc.vector.bn_aggr(mv[:, par, t, :], stats[:, t, :]))
                    st.wait()
                    dve.sem_inc(s_stat, 1)
                    if not first:
                        reduce(i - 1, 1 - par)
                    dve.wait_ge(s_root, i + 1)
                    st.mark(nc.vector.reciprocal(cols[:, par, 0, :], root[:, par, :]))
                    st.wait()
                    st.mark(nc.vector.scalar_tensor_tensor(cols[:, par, 1, :], mv[:, par, :, 0], -1.0,
                                                           cols[:, par, 0, :], ALU.mult, ALU.mult))
                    st.wait()
                    dve.sem_inc(s_cols, 1)

                chunk_loop(dve, chunk, NCH, st, DV)
                reduce(NCH - 1, 0)
                st.wait()
                st.mark(nc.vector.tensor_tensor(occ[:], within[:], before[:], ALU.add))
                st.wait()

            @block.tensor
            def _(pe):
                def column(j, q, par2, start=False):
                    pe.wait_ge(s_hot, j + 1)
                    pe.wait_ge(s_hotc, j)
                    nc.tensor.transpose(psT[:], hot_lo[:, q, :], identb[:]).then_inc(s_hotT, 1)
                    pe.wait_ge(s_run, j + 1)
                    nc.tensor.matmul(psC[:], hot_lo[:, q, :], hot_hi[:, par2, q, :], start=start, stop=True,
                                     skip_group_check=True).then_inc(s_cnt, 1)
                    pe.wait_ge(s_hotc, j + 1)
                    pe.wait_ge(s_red, j + 1)
                    nc.tensor.matmul(psL[q][:], hotT[:, q % 2, :], cnt_lo[:, q % 2, :], start=True, stop=True
                                     ).then_inc(s_look, 1)

                def chunk(i, par, use):
                    for q in range(EQ):
                        column(EQ * i + q, q, par, isinstance(i, int) and i == q == 0)

                chunk_loop(pe, chunk)

            @block.scalar
            def _(act):
                for par in range(2):
                    act.sem_inc(s_xfree[par], 1)
                hf = h_tab[0].rearrange("(c p t) f -> c p (t f)", p=P, t=RT)

                def chunk(i, par, use):
                    def column(q):
                        j = EQ * i + q
                        act.wait_ge(s_hotT, j + 1)
                        nc.scalar.activation(hotT[:, q % 2, :], psT[:], ACT.Copy).then_inc(s_hotc, 1)
                        act.wait_ge(s_cnt, j + 1)
                        nc.scalar.activation(cnt_lo[:, (q + 1) % 2, :], psC[:], ACT.Copy).then_inc(s_run, 1)

                    column(0)
                    column(1)
                    act.wait_ge(s_stat, i + 1)
                    nc.scalar.activation(root[:, par], mv[:, par, :, 1], ACT.Sqrt, bias=epsc[:, 0:1]
                                         ).then_inc(s_root, 1)
                    column(2)
                    column(3)
                    act.wait_ge(s_cols, i + 1)
                    need(act, s_hout[par], 16 * use)
                    for t in range(RT):
                        nc.scalar.activation(hb[par][:, t, :], xb[par][:, t, :], ACT.Relu,
                                             bias=cols[:, par, 1, t:t + 1], scale=cols[:, par, 0, t:t + 1]
                                             ).then_inc(s_rows, 1)
                    act.wait_ge(s_rows, RT * (i + 1))
                    act.sem_inc(s_xfree[par], 1)
                    act.dma_start(hf[bass.ds(i, 1)].rearrange("c p n -> (c p) n"),
                                  hb[par][:].rearrange("p t f -> p (t f)")).then_inc(s_hout[par], 16)

                chunk_loop(act, chunk)
                act.wait_ge(s_hout[0], 16 * (NCH // 2 + 1))
                act.wait_ge(s_hout[1], 16 * (NCH // 2))

        s_dv3 = sem("s3_dve")
        s_pe3 = sem("s3_pe")
        s_out3 = sem("s3_out")
        node_look = sb("node_look", [P, HI, 2], I32)
        pay0 = sb("pay0", [P, EC, 2], I32)
        c3 = ExitStack()
        with c3:
            has = sb("has", [P, HI], F32, c3)
            ones_w = sb("ones_w", [P, HI], F32, c3)
            upto_hi = sb("upto_hi", [P, 2, HI], F32, c3)
            rank = sb("rank", [P, 2, HI], F32, c3)
            late = sb("late", [P, HI], F32, c3)
            ps = [pb(f"ps3_{i}", [P, HI], F32, c3) for i in range(4)]
            block = c3.enter_context(nc.Block())

            @block.vector
            def _(dve):
                st = Steps(dve, s_dv3)
                st.mark(nc.vector.tensor_scalar(has[:], cnt_lo[:, 0], 0.0, None, ALU.is_gt))
                st.mark(nc.vector.memset(ones_w[:], 1.0))
                st.mark(nc.vector.memset(pay0[:, :, 0], 0))
                st.mark(nc.vector.memset(pay0[:, :, 1], -FAR))
                st.mark(nc.vector.tensor_scalar(late[:], iota_w[:], float(LO), iota_p[:, 0:1], ALU.mult, ALU.add))
                st.wait()
                dve.wait_ge(s_pe3, 4)
                for q in range(2):
                    st.mark(nc.vector.tensor_tensor_scan(upto_hi[:, q], ones_w[:], ps[2 * q][:], 0.0,
                                                         ALU.mult, ALU.add))
                    st.wait()
                    st.mark(nc.vector.tensor_tensor(rank[:, q], upto_hi[:, q], ps[2 * q][:], ALU.subtract))
                    st.wait()
                    st.mark(nc.vector.tensor_tensor(rank[:, q], rank[:, q], ps[2 * q + 1][:], ALU.add))
                    st.wait()
                st.mark(nc.vector.tensor_tensor(late[:], late[:], rank[:, 1], ALU.subtract))
                st.wait()
                st.mark(nc.vector.tensor_scalar(late[:], late[:], upto_hi[:, 1, HI - 1:HI], None, ALU.add))
                st.wait()
                st.mark(nc.vector.tensor_tensor(rank[:, 1], rank[:, 1], late[:], ALU.subtract))
                st.wait()
                st.mark(nc.vector.tensor_tensor(rank[:, 1], rank[:, 1], has[:], ALU.mult))
                st.wait()
                st.mark(nc.vector.tensor_tensor(rank[:, 1], rank[:, 1], late[:], ALU.add))
                st.wait()
                st.mark(nc.vector.tensor_scalar(late[:], rank[:, 1], float(EPAD), float(-NPAD), ALU.is_ge, ALU.mult))
                st.wait()
                st.mark(nc.vector.tensor_scalar(rank[:, 1], rank[:, 1], float(EPAD), None, ALU.add))
                st.wait()
                st.mark(nc.vector.tensor_tensor(rank[:, 1], rank[:, 1], late[:], ALU.add))
                st.wait()
                st.mark(nc.vector.tensor_copy(node_look[:, :, 0], rank[:, 0]))
                st.mark(nc.vector.tensor_copy(node_look[:, :, 1], rank[:, 1]))
                st.mark(nc.vector.tensor_copy(node_pos[:], rank[:, 1]))
                st.wait()

            @block.tensor
            def _(pe):
                pe.wait_ge(s_dv3, 1)
                for q, m in enumerate((cnt_lo[:, 0], has[:])):
                    nc.tensor.matmul(ps[2 * q][:], ones[:], m, start=True, stop=True).then_inc(s_pe3, 1)
                    nc.tensor.matmul(ps[2 * q + 1][:], later[:], m, start=True, stop=True).then_inc(s_pe3, 1)

            @block.sync
            def _(sp):
                sp.wait_ge(s_dv3, 5)
                sp.dma_start(sort_tab.rearrange("(p j) w -> p j w", j=EC), pay0[:]).then_inc(s_out3, 16)
                sp.wait_ge(s_dv3, 22)
                sp.dma_start(node_tab.rearrange("(p j) w -> p j w", j=HI), node_look[:]).then_inc(s_out3, 16)
                sp.wait_ge(s_out3, 32)

        def pool_columns(pool, name, cbuf, table, idx, cols, scatter):
            s_cp = sem(name + "_cp")
            s_dma = [sem(name + "_d0"), sem(name + "_d1")]
            s_tk = sem(name + "_tk")
            ib = sb(name + "_ib", [P, 2, JG], I32, cbuf)
            rb = sb(name + "_rb", [P, 2, JG, 2], I32, cbuf)
            st = Steps(pool, s_cp)
            def group(i, par, use):
                pool.wait_ge(s_dma[par], 16 * JG * use)
                if not scatter:
                    take(i - 2, par)
                st.mark(nc.gpsimd.tensor_copy(ib[:, par], idx[:, bass.ds(JG * i, JG)]))
                if scatter:
                    st.mark(nc.gpsimd.tensor_copy(rb[:, par], cols[:, bass.ds(JG * i, JG), :]))
                st.wait()
                pool.sem_inc(s_tk, 1)
                issue(par)

            def take(i, par):
                st.mark(nc.gpsimd.tensor_copy(cols[:, bass.ds(JG * i, JG), :], rb[:, par]))
                st.wait()

            def issue(par):
                for q in range(JG):
                    if scatter:
                        pool.indirect_dma_start(table, bass.IndirectOffsetOnAxis(ap=ib[:, par, q:q + 1], axis=0),
                                                rb[:, par, q, :], None, bounds_check=EPAD - 1, oob_is_err=False
                                                ).then_inc(s_dma[par], 16)
                    else:
                        pool.indirect_dma_start(rb[:, par, q, :], None, table,
                                                bass.IndirectOffsetOnAxis(ap=ib[:, par, q:q + 1], axis=0)
                                                ).then_inc(s_dma[par], 16)

            for i in range(2):
                st.mark(nc.gpsimd.tensor_copy(ib[:, i], idx[:, JG * i:JG * (i + 1)]))
                if scatter:
                    st.mark(nc.gpsimd.tensor_copy(rb[:, i], cols[:, JG * i:JG * (i + 1), :]))
                st.wait()
                pool.sem_inc(s_tk, 1)
                issue(i)

            def both(k):
                group(2 * k + 2, 0, k + 1)
                group(2 * k + 3, 1, k + 1)

            engine_loop(pool, NG // 2 - 1, both, st, 4)
            for par in range(2):
                pool.wait_ge(s_dma[par], 16 * JG * (NG // 2))
                if not scatter:
                    take(NG - 2 + par, par)

        def convolve(layer):
            n = f"cv{layer}_"
            s_m = [sem(n + "m0"), sem(n + "m1")]
            s_m0 = sem(n + "m_first")
            s_done = sem(n + "m_done")
            s_halo = sem(n + "halo")
            s_fb = sem(n + "blank")
            s_fbf = sem(n + "blank_free")
            s_dv = sem(n + "dve")
            s_o = sem(n + "out")
            s_sc = [sem(n + "sc0"), sem(n + "sc1")]
            s_cp = sem(n + "cp")
            s_tk = sem(n + "tick")
            c = ExitStack()
            with c:
                M = [sb(f"{n}M{i}", [P, JG + 3, D], F32, c) for i in range(2)]
                S1 = [sb(f"{n}S{i}", [P, JG + 2, D], F32, c) for i in range(2)]
                L2 = [sb(f"{n}L{i}", [P, JG, D], F32, c) for i in range(2)]
                H2 = [sb(f"{n}H{i}", [P, JG, D], F32, c) for i in range(2)]
                low = sb(n + "low", [P, JG + 2, D], F32, c)
                high = sb(n + "high", [P, JG + 2, D], F32, c)
                A = sb(n + "A", [P, JG, D], F32, c)
                ob = [sb(f"{n}ob{i}", [P, JG, D], F32, c) for i in range(2)]
                ms1 = sb(n + "ms1", [P, 2, JG + 2], I32, c)
                ms2 = sb(n + "ms2", [P, 2, JG], I32, c)
                gi = sb(n + "gi", [P, 2, JG], I32, c)
                pi = sb(n + "pi", [P, 2, JG], I32, c)
                block = c.enter_context(nc.Block())

                @block.gpsimd
                def _(pool):
                    st = Steps(pool, s_cp)
                    for q in range(3):
                        pool.indirect_dma_start(M[0][:, q, :], None, h_tab[layer],
                                                bass.IndirectOffsetOnAxis(ap=gat_src[:, q:q + 1], axis=0)
                                                ).then_inc(s_m0, 16)

                    def gather(i, par):
                        pool.wait_ge(s_done, i + 1)
                        pool.wait_ge(s_halo, i + 1)
                        st.mark(nc.gpsimd.tensor_copy(gi[:, par], gat_src[:, bass.ds(JG * i + 3, JG)]))
                        st.wait()
                        pool.sem_inc(s_tk, 1)
                        for q in range(JG):
                            pool.indirect_dma_start(M[par][:, 3 + q, :], None, h_tab[layer],
                                                    bass.IndirectOffsetOnAxis(ap=gi[:, par, q:q + 1], axis=0)
                                                    ).then_inc(s_m[par], 16)

                    def scatter(i, par, use):
                        need(pool, s_sc[par], 16 * JG * use)
                        st.mark(nc.gpsimd.tensor_copy(pi[:, par], put_idx[:, bass.ds(JG * i, JG)]))
                        st.wait()
                        pool.wait_ge(s_o, i + 1)
                        pool.sem_inc(s_tk, 1)
                        for q in range(JG):
                            pool.indirect_dma_start(o_tab[layer],
                                                    bass.IndirectOffsetOnAxis(ap=pi[:, par, q:q + 1], axis=0),
                                                    ob[par][:, q, :], None, bounds_check=N - 1, oob_is_err=False
                                                    ).then_inc(s_sc[par], 16)

                    def group(i, par, use):
                        gather(i, par)
                        if not isinstance(i, int) or i:
                            scatter(i - 1, 1 - par, use + par - 1)

                    chunk_loop(pool, group, NG, st, 2)
                    scatter(NG - 1, 1, NG // 2 - 1)
                    for par in range(2):
                        pool.wait_ge(s_sc[par], 16 * JG * (NG // 2))

                @block.scalar
                def _(act):
                    act.sem_inc(s_halo, 2)
                    bl = blank_p[layer][:].unsqueeze(1)

                    def group(i, par, use):
                        act.wait_ge(s_fbf, i + 1)
                        nc.scalar.activation(S1[par][:], bl.to_broadcast([P, JG + 2, D]), ACT.Copy).then_inc(s_fb, 1)
                        nc.scalar.activation(L2[par][:], bl.to_broadcast([P, JG, D]), ACT.Copy).then_inc(s_fb, 1)
                        nc.scalar.activation(H2[par][:], bl.to_broadcast([P, JG, D]), ACT.Copy).then_inc(s_fb, 1)
                        nc.scalar.activation(ms1[:, par], same1[:, bass.ds(JG * i, JG + 2)], ACT.Copy
                                             ).then_inc(s_fb, 1)
                        nc.scalar.activation(ms2[:, par], same2[:, bass.ds(JG * i, JG)], ACT.Copy).then_inc(s_fb, 1)
                        if not isinstance(i, int) or i:
                            act.wait_ge(s_m[1 - par], 16 * JG * (use + (1 if par == 1 else 0)))
                            act.wait_ge(s_done, i + 1)
                            nc.scalar.activation(M[par][:, 0:3, :], M[1 - par][:, JG:JG + 3, :], ACT.Copy
                                                 ).then_inc(s_halo, 1)

                    chunk_loop(act, group, NG)

                @block.vector
                def _(dve):
                    st = Steps(dve, s_dv)
                    dve.sem_inc(s_done, 2)
                    dve.sem_inc(s_fbf, 2)
                    cw, cb = cwb[layer], cbb[layer]
                    tt = nc.vector.tensor_tensor

                    def group(i, par, use):
                        dve.wait_ge(s_fb, 5 * (i + 1))
                        dve.wait_ge(s_m[par], 16 * JG * (use + 1))
                        dve.wait_ge(s_halo, i + 2)
                        dve.sem_inc(s_tk, 1)
                        st.mark(nc.vector.copy_predicated(
                            S1[par][:], ms1[:, par].unsqueeze(2).to_broadcast([P, JG + 2, D]), M[par][:, 1:JG + 3, :]))
                        st.wait()
                        st.mark(tt(low[:], M[par][:, 0:JG + 2, :], S1[par][:], ALU.min))
                        st.mark(tt(high[:], M[par][:, 0:JG + 2, :], S1[par][:], ALU.max))
                        st.wait()
                        dve.sem_inc(s_done, 1)
                        mask = ms2[:, par].unsqueeze(2).to_broadcast([P, JG, D])
                        st.mark(nc.vector.copy_predicated(L2[par][:], mask, low[:, 2:JG + 2, :]))
                        st.mark(nc.vector.copy_predicated(H2[par][:], mask, high[:, 2:JG + 2, :]))
                        need(dve, s_sc[par], 16 * JG * use)
                        st.wait()
                        dve.sem_inc(s_tk, 1)
                        lo14, hi14 = low[:, 0:JG, :], high[:, 0:JG, :]
                        st.mark(tt(ob[par][:], lo14, L2[par][:], ALU.min))
                        st.mark(tt(A[:], lo14, L2[par][:], ALU.max))
                        st.wait()
                        st.mark(tt(L2[par][:], hi14, H2[par][:], ALU.min))
                        st.wait()
                        st.mark(tt(H2[par][:], hi14, H2[par][:], ALU.max))
                        st.mark(tt(lo14, A[:], L2[par][:], ALU.min))
                        st.wait()
                        st.mark(tt(A[:], A[:], L2[par][:], ALU.max))
                        st.mark(nc.vector.tensor_scalar(ob[par][:], ob[par][:], cw[:, 0:1], cb[:, 0:1],
                                                        ALU.mult, ALU.add))
                        for q, v in enumerate((lo14, A[:], H2[par][:])):
                            st.wait()
                            st.mark(nc.vector.scalar_tensor_tensor(ob[par][:], v, cw[:, q + 1:q + 2], ob[par][:],
                                                                   ALU.mult, ALU.add))
                        st.wait()
                        dve.sem_inc(s_o, 1)
                        dve.sem_inc(s_fbf, 1)

                    group_marks = 15

                    dve.wait_ge(s_m0, 48)
                    chunk_loop(dve, group, NG, st, group_marks)

        def statistics(layer, pool_work=None):
            n = f"st{layer}_"
            s_in = [sem(n + "in0"), sem(n + "in1")]
            s_fr = [sem(n + "fr0"), sem(n + "fr1")]
            s_u = sem(n + "u")
            s_q = sem(n + "q")
            s_pe = sem(n + "pe")
            s_dv = sem(n + "dve")
            s_rt = sem(n + "rt")
            c = ExitStack()
            with c:
                hb = [sb(f"{n}h{i}", [P, RT * D], F32, c) for i in range(2)]
                ob = [sb(f"{n}o{i}", [P, RT * D], F32, c) for i in range(2)]
                sq = [sb(f"{n}q{i}", [P, RT * D], F32, c) for i in range(2)]
                tot = sb(n + "tot", [P, 2, D], F32, c)
                var = sb(n + "var", [P, D], F32, c)
                rt = sb(n + "rt", [P, D], F32, c)
                psU = pb(n + "psU", [P, 512], F32, c)
                psQ = pb(n + "psQ", [P, 512], F32, c)
                block = c.enter_context(nc.Block())
                hv = h_tab[layer].rearrange("(c p t) f -> c p (t f)", p=P, t=RT)
                ov = o_tab[layer].rearrange("(c p t) f -> c p (t f)", p=P, t=RT)

                @block.sync
                def _(sp):
                    def load(i, par, use):
                        sp.wait_ge(s_fr[par], use + 1)
                        for t, v in ((hb, hv), (ob, ov)):
                            sp.dma_start(t[par][:], v[bass.ds(i, 1)].rearrange("c p n -> (c p) n")
                                         ).then_inc(s_in[par], 16)

                    chunk_loop(sp, load)

                if pool_work:
                    @block.gpsimd
                    def _(pool):
                        pool_work(pool, c)

                @block.vector
                def _(dve):
                    st = Steps(dve, s_dv)

                    def chunk(i, par, use):
                        dve.wait_ge(s_in[par], 32 * (use + 1))
                        nc.vector.scalar_tensor_tensor(ob[par][:], hb[par][:], ab[layer][:, 0:1], ob[par][:],
                                                       ALU.mult, ALU.add).then_inc(s_u, 1)

                    chunk_loop(dve, chunk)
                    dve.wait_ge(s_pe, NCH)
                    for q, ps in enumerate((psU, psQ)):
                        st.mark(nc.vector.tensor_reduce(tot[:, q, :], ps[:].rearrange("p (t f) -> p f t", f=D),
                                                        AX.X, ALU.add))
                    st.wait()
                    st.mark(nc.vector.tensor_scalar(tot[:], tot[:], 1.0 / N, None, ALU.mult))
                    st.wait()
                    st.mark(nc.vector.tensor_tensor(var[:], tot[:, 0, :], tot[:, 0, :], ALU.mult))
                    st.wait()
                    st.mark(nc.vector.tensor_tensor(var[:], tot[:, 1, :], var[:], ALU.subtract))
                    st.wait()
                    st.mark(nc.vector.tensor_scalar(var[:], var[:], 0.0, None, ALU.max))
                    st.wait()
                    dve.wait_ge(s_rt, 1)
                    st.mark(nc.vector.reciprocal(rt[:], rt[:]))
                    st.wait()
                    st.mark(nc.vector.tensor_tensor(bn_s[layer][:], rt[:], gb[layer][:], ALU.mult))
                    st.wait()
                    st.mark(nc.vector.tensor_tensor(var[:], tot[:, 0, :], bn_s[layer][:], ALU.mult))
                    st.wait()
                    st.mark(nc.vector.tensor_tensor(bn_t[layer][:], beb[layer][:], var[:], ALU.subtract))
                    st.wait()

                @block.scalar
                def _(act):
                    def chunk(i, par, use):
                        act.wait_ge(s_u, i + 1)
                        act.wait_ge(s_fr[par], use + 1)
                        nc.scalar.activation(sq[par][:], ob[par][:], ACT.Square).then_inc(s_q, 1)

                    chunk_loop(act, chunk)
                    act.wait_ge(s_dv, 6)
                    nc.scalar.activation(rt[:], var[:], ACT.Sqrt, bias=epsc[:, 0:1]).then_inc(s_rt, 1)

                @block.tensor
                def _(pe):
                    for par in range(2):
                        pe.sem_inc(s_fr[par], 1)

                    def chunk(i, par, use):
                        first, last = (isinstance(i, int) and i == v for v in (0, NCH - 1))
                        w = ones_last if last else ones
                        for t, s, ps in ((ob, s_u, psU), (sq, s_q, psQ)):
                            pe.wait_ge(s, i + 1)
                            for q in range(2):
                                ins = nc.tensor.matmul(ps[:], w[:], t[par][:, 512 * q:512 * (q + 1)],
                                                       start=first and q == 0, stop=last and q == 1,
                                                       skip_group_check=True)
                        ins.then_inc(s_pe, 1)
                        pe.wait_ge(s_pe, i + 1)
                        pe.sem_inc(s_fr[par], 1)

                    chunk_loop(pe, chunk)

        bn_s = [sb(f"bn_s{i}", [P, D]) for i in range(2)]
        bn_t = [sb(f"bn_t{i}", [P, D]) for i in range(2)]

        def apply0(pool_work):
            s_in = [sem("ap_in0"), sem("ap_in1")]
            s_out = [sem("ap_out0"), sem("ap_out1")]
            s_dv = sem("ap_dve")
            s_r = sem("ap_rows")
            c = ExitStack()
            with c:
                hb = [sb(f"ap_h{i}", [P, RT, D], F32, c) for i in range(2)]
                ob = [sb(f"ap_o{i}", [P, RT, D], F32, c) for i in range(2)]
                block = c.enter_context(nc.Block())
                hv, ov, wv = (t.rearrange("(c p t) f -> c p t f", p=P, t=RT) for t in (h_tab[0], o_tab[0], h_tab[1]))

                @block.sync
                def _(sp):
                    def load(i, par, use):
                        need(sp, s_out[par], 16 * use)
                        for t, v in ((hb, hv), (ob, ov)):
                            sp.dma_start(t[par][:], v[bass.ds(i, 1)].rearrange("c p t f -> (c p) t f")
                                         ).then_inc(s_in[par], 16)

                    chunk_loop(sp, load)

                @block.gpsimd
                def _(pool):
                    pool_work(pool, c)

                @block.scalar
                def _(act):
                    def store(i, par, use):
                        act.wait_ge(s_r, i + 1)
                        act.dma_start(wv[bass.ds(i, 1)].rearrange("c p t f -> (c p) t f"), ob[par][:]
                                      ).then_inc(s_out[par], 16)

                    chunk_loop(act, store)
                    act.wait_ge(s_out[0], 16 * (NCH // 2 + 1))
                    act.wait_ge(s_out[1], 16 * (NCH // 2))

                @block.vector
                def _(dve):
                    st = Steps(dve, s_dv)
                    sc = bn_s[0][:].unsqueeze(1).to_broadcast([P, RT, D])
                    sh = bn_t[0][:].unsqueeze(1).to_broadcast([P, RT, D])

                    def chunk(i, par, use):
                        dve.wait_ge(s_in[par], 32 * (use + 1))
                        normalise(nc, st, hb[par], ob[par][:], ab[0], sc, sh)
                        st.wait()
                        dve.sem_inc(s_r, 1)

                    chunk_loop(dve, chunk, NCH, st, 4)

        def apply1():
            s_in = [sem("a1_in0"), sem("a1_in1")]
            s_out = [sem("a1_out0"), sem("a1_out1")]
            s_free = sem("a1_free")
            s_dv = sem("a1_dve")
            s_r = sem("a1_rows")
            s_cp = sem("a1_cp")
            s_tk = sem("a1_tk")
            s_pad = sem("a1_pad")
            c = ExitStack()
            with c:
                xb = [sb(f"a1_x{i}", [P, RT, D], F32, c) for i in range(2)]
                hb = [sb(f"a1_h{i}", [P, RT, D], F32, c) for i in range(2)]
                ob = [sb(f"a1_o{i}", [P, RT, D], F32, c) for i in range(2)]
                rb = [sb(f"a1_r{i}", [P, RT, IDW], F32, c) for i in range(2)]
                number = sb("a1_number", [P, RT], F32, c)
                pi = sb("a1_pi", [P, 2, RT], I32, c)
                block = c.enter_context(nc.Block())
                hv, ov = (t.rearrange("(c t p) f -> c p t f", p=P, t=RT) for t in (h_tab[1], o_tab[1]))
                m = (NCH - 1) * P * RT
                xv = x[0:m, :].rearrange("(c t p) f -> c p t f", p=P, t=RT)
                full = (N - m) // P
                part = N - m - full * P

                @block.sync
                def _(sp):
                    def load(i, par, use):
                        last = isinstance(i, int) and i == NCH - 1
                        sp.wait_ge(s_free, i + 1)
                        for t, v in ((hb, hv), (ob, ov)) + (() if last else ((xb, xv),)):
                            sp.dma_start(t[par][:], v[bass.ds(i, 1)].rearrange("c p t f -> (c p) t f")
                                         ).then_inc(s_in[par], 16)
                        if last:
                            sp.wait_ge(s_pad, 1)
                            sp.dma_start(xb[par][:, 0:full, :], x[m:m + full * P, :].rearrange("(t p) f -> p t f", p=P)
                                         ).then_inc(s_in[par], 16)
                            sp.dma_start(xb[par][0:part, full, :], x[m + full * P:N, :]).then_inc(s_in[par], 16)

                    chunk_loop(sp, load)

                @block.vector
                def _(dve):
                    st = Steps(dve, s_dv)
                    sc = bn_s[1][:].unsqueeze(1).to_broadcast([P, RT, D])
                    sh = bn_t[1][:].unsqueeze(1).to_broadcast([P, RT, D])
                    st.mark(nc.vector.tensor_scalar(number[:], iota_w[:, 0:RT], float(P), iota_p[:, 0:1],
                                                    ALU.mult, ALU.add))
                    for par in range(2):
                        st.mark(nc.vector.memset(rb[par][:, :, D:IDW], 0.0))
                    st.wait()
                    dve.sem_inc(s_free, 2)

                    def chunk(i, par, use):
                        last = isinstance(i, int) and i == NCH - 1
                        dve.wait_ge(s_in[par], 48 * (use + 1) + (16 if last else 0))
                        need(dve, s_out[par], 16 * RT * use)
                        st.mark(nc.vector.tensor_copy(rb[par][:, :, D].bitcast(I32), number[:]))
                        normalise(nc, st, hb[par], ob[par][:], ab[1], sc, sh)
                        st.mark(nc.vector.tensor_scalar(number[:], number[:], float(P * RT), None, ALU.add))
                        st.wait()
                        st.mark(nc.vector.tensor_tensor(rb[par][:, :, 0:D], ob[par][:], xb[par][:], ALU.add))
                        st.wait()
                        dve.sem_inc(s_r, 1)
                        dve.sem_inc(s_free, 1)

                    chunk_loop(dve, chunk, NCH, st, 7)

                @block.gpsimd
                def _(pool):
                    st = Steps(pool, s_cp)
                    def chunk(i, par, use):
                        if isinstance(i, int) and i == NCH - 1:
                            pool.wait_ge(s_free, NCH - 2 + 1)
                            nc.gpsimd.memset(xb[0][:], 0.0).then_inc(s_pad, 1)
                        need(pool, s_out[par], 16 * RT * use)
                        st.mark(nc.gpsimd.tensor_copy(pi[:, par], node_pos[:, bass.ds(RT * i, RT)]))
                        st.wait()
                        pool.wait_ge(s_r, i + 1)
                        pool.sem_inc(s_tk, 1)
                        for t in range(RT):
                            pool.indirect_dma_start(x2_tab, bass.IndirectOffsetOnAxis(ap=pi[:, par, t:t + 1], axis=0),
                                                    rb[par][:, t, :], None).then_inc(s_out[par], 16)

                    chunk_loop(pool, chunk, NCH, st, 1)
                    pool.wait_ge(s_out[0], 16 * RT * (NCH // 2 + 1))
                    pool.wait_ge(s_out[1], 16 * RT * (NCH // 2))

        convolve(0)
        statistics(0, lambda pool, c: pool_columns(pool, "lks", c, node_tab, src_at, look, False))
        apply0(lambda pool, c: pool_columns(pool, "lkd", c, node_tab, dst_at, pair, False))
        s_dv4 = sem("s4_dve")
        c4 = ExitStack()
        with c4:
            pf = sb("pf", [P, EC], F32, c4)
            pi4 = sb("pi4", [P, EC], I32, c4)
            pj4 = sb("pj4", [P, EC], I32, c4)
            pg = sb("pg", [P, EC], F32, c4)
            ph = sb("ph", [P, EC], F32, c4)
            block = c4.enter_context(nc.Block())

            @block.vector
            def _(dve):
                st = Steps(dve, s_dv4)

                def do(ins):
                    st.mark(ins)
                    st.wait()

                do(nc.vector.tensor_copy(pf[:], look[:, :, 0]))
                do(nc.vector.tensor_tensor(pf[:], pf[:], occ[:], ALU.add))
                do(nc.vector.tensor_copy(pi4[:], pf[:]))
                do(nc.vector.tensor_scalar(pj4[:], pi4[:], P - 1, None, ALU.bitwise_and))
                do(nc.vector.tensor_copy(pg[:], pj4[:]))
                do(nc.vector.tensor_scalar(pj4[:], pi4[:], 7, None, ALU.logical_shift_right))
                do(nc.vector.tensor_copy(ph[:], pj4[:]))
                do(nc.vector.scalar_tensor_tensor(pf[:], pg[:], float(EC), ph[:], ALU.mult, ALU.add))
                do(nc.vector.tensor_copy(pg[:], edge_src[:, 0:EC]))
                do(nc.vector.tensor_scalar(pg[:], pg[:], float(NPAD), None, ALU.is_ge))
                do(nc.vector.scalar_tensor_tensor(sort_at[:], pg[:], float(FAR), pf[:], ALU.mult, ALU.add))
                do(nc.vector.tensor_copy(pair[:, :, 0], pair[:, :, 1]))
                do(nc.vector.tensor_copy(pair[:, :, 1], look[:, :, 1]))
        convolve(1)
        statistics(1, lambda pool, c: pool_columns(pool, "srt", c, sort_tab, sort_at, pair, True))
        apply1()
        W_msg, b_msg, W_ih, W_hh, b_ih, b_hh = gru

        wih = sb("wih", [P, 3 * D])
        whh = sb("whh", [P, 3 * D])
        wmsg = sb("wmsg", [P, D])
        bmsg = sb("bmsg", [P, D])
        bih = sb("bih", [P, 3])
        bhh = sb("bhh", [P, 3])
        brz = sb("brz", [P, 2])
        agg = sb("agg", [P, EPAD + CW])
        sorted_ = sb("sorted", [P, EC, 2], I32)
        base = sb("base", [1, EC], I32)
        lrank = sb("lrank", [P, EC])
        srow = sb("srow", [P, EC], I32)
        s_hst = [sem("g_hst0"), sem("g_hst1")]
        s_mst = [sem("g_mst0"), sem("g_mst1")]
        NPC = NPAD // CW
        TPC = CW // P
        x2v = x2_tab.rearrange("(c p t) w -> c p t w", p=P, t=TPC)
        htv = ht_tab.rearrange("f (c n) -> f c n", n=CW)
        msgv = [t.rearrange("(c p t) f -> c p (t f)", p=P, t=TPC) for t in msg_tab]

        s_w = sem("i_w")
        s_xin = [sem("i_x0"), sem("i_x1")]
        s_stat = sem("i_stat")
        s_root = sem("i_root")
        s_cols = sem("i_cols")
        s_relu = sem("i_relu")
        s_tr = sem("i_tr")
        s_hT = sem("i_hT")
        s_pm = sem("i_pm")
        s_me = sem("i_me")
        s_dv = sem("i_dve")
        s_srt = sem("i_sorted")
        s_pl = sem("i_pool")
        s_tk = sem("i_tick")
        c5 = ExitStack()
        with c5:
            xb = [sb(f"i_x{i}", [P, TPC, IDW], F32, c5) for i in range(2)]
            rb = [sb(f"i_r{i}", [P, TPC, D], F32, c5) for i in range(2)]
            hT = [sb(f"i_hT{i}", [P, CW], F32, c5) for i in range(2)]
            mb = [sb(f"i_m{i}", [P, TPC, D], F32, c5) for i in range(2)]
            stats = sb("i_stats", [P, TPC, 6], F32, c5)
            mv = sb("i_mv", [P, 2, TPC, 2], F32, c5)
            root = sb("i_root", [P, 2, TPC], F32, c5)
            cols = sb("i_cols", [P, 2, 2, TPC], F32, c5)
            rankf = sb("i_rank", [P, EC], F32, c5)
            psT = [pb(f"i_psT{i}", [P, TPC, P], F32, c5) for i in range(2)]
            psM = [pb(f"i_psM{i}", [P, TPC, D], F32, c5) for i in range(2)]
            psR = pb("i_psR", [P, EC], F32, c5)
            block = c5.enter_context(nc.Block())

            @block.sync
            def _(sp):
                loads = [sp.dma_start(sorted_[:], sort_tab.rearrange("(p j) w -> p j w", j=EC)),
                         sp.dma_start(wih[:], W_ih), sp.dma_start(whh[:], W_hh), sp.dma_start(wmsg[:], W_msg),
                         sp.dma_start(bmsg[:], b_msg.partition_broadcast(P))]
                for t, v in ((bih, b_ih), (bhh, b_hh)):
                    loads.append(sp.dma_start(t[:], v.rearrange("(g p) -> p g", p=P), allow_slow_non_contiguous=True))
                for ins in loads:
                    ins.then_inc(s_w, 16)

                def chunk(i, par, use):
                    need(sp, s_relu, TPC * (i - 1))
                    sp.dma_start(xb[par][:], x2v[bass.ds(i, 1)].rearrange("c p t w -> (c p) t w")
                                 ).then_inc(s_xin[par], 16)
                    if not isinstance(i, int) or i >= 2:
                        store_h(i - 2, par)
                    if not isinstance(i, int) or i >= 3:
                        store_m(i - 3, 1 - par)

                def store_h(i, par):
                    sp.wait_ge(s_hT, i + 1)
                    sp.dma_start(htv[:, bass.ds(i, 1), :].rearrange("f c n -> f (c n)"), hT[par][:]
                                 ).then_inc(s_hst[par], 16)

                def store_m(i, par):
                    sp.wait_ge(s_me, i + 1)
                    sp.dma_start(msgv[0][bass.ds(i, 1)].rearrange("c p n -> (c p) n"),
                                 mb[par][:].rearrange("p t f -> p (t f)")).then_inc(s_mst[par], 16)

                chunk_loop(sp, chunk, NPC, peel=4)
                store_h(NPC - 2, 0)
                store_m(NPC - 3, 1)
                store_h(NPC - 1, 1)
                store_m(NPC - 2, 0)
                store_m(NPC - 1, 1)
                for par in range(2):
                    sp.wait_ge(s_hst[par], 16 * (NPC // 2))
                    sp.wait_ge(s_mst[par], 16 * (NPC // 2))

            @block.gpsimd
            def _(pool):
                nc.gpsimd.memset(agg[:], 0.0).then_inc(s_pl, 1)

            @block.vector
            def _(dve):
                st = Steps(dve, s_dv)

                def do(ins):
                    st.mark(ins)
                    st.wait()

                dve.wait_ge(s_w, 16 * 7)
                do(nc.vector.tensor_tensor(brz[:], bih[:, 0:2], bhh[:, 0:2], ALU.add))
                do(nc.vector.tensor_copy(srow[:], sorted_[:, :, 0]))
                do(nc.vector.tensor_copy(rankf[:], sorted_[:, :, 1]))
                do(nc.vector.tensor_scalar(rankf[:], rankf[:], float(-EPAD), None, ALU.add))
                do(nc.vector.tensor_copy(base[:], rankf[0:1, :]))
                dve.sem_inc(s_srt, 1)
                dve.wait_ge(s_srt, 2)
                do(nc.vector.tensor_tensor(lrank[:], rankf[:], psR[:], ALU.subtract))

                def evacuate(i, par, use):
                    dve.wait_ge(s_pm, i + 1)
                    need(dve, s_mst[par], 16 * use)
                    nc.vector.tensor_tensor(mb[par][:], psM[par][:], bmsg[:].unsqueeze(1).to_broadcast([P, TPC, D]),
                                            ALU.add).then_inc(s_me, 1)

                def chunk(i, par, use):
                    dve.wait_ge(s_xin[par], 16 * (use + 1))
                    for t in range(TPC):
                        st.mark(nc.vector.bn_stats(stats[:, t, :], xb[par][:, t, 0:D]))
                    st.wait()
                    dve.sem_inc(s_tk, 1)
                    for t in range(TPC):
                        st.mark(nc.vector.bn_aggr(mv[:, par, t, :], stats[:, t, :]))
                    st.wait()
                    dve.sem_inc(s_stat, 1)
                    if not isinstance(i, int) or i >= 2:
                        evacuate(i - 2, *behind(par, use, 2))
                    dve.wait_ge(s_root, i + 1)
                    st.mark(nc.vector.reciprocal(cols[:, par, 0, :], root[:, par, :]))
                    st.wait()
                    st.mark(nc.vector.scalar_tensor_tensor(cols[:, par, 1, :], mv[:, par, :, 0], -1.0,
                                                           cols[:, par, 0, :], ALU.mult, ALU.mult))
                    st.wait()
                    dve.sem_inc(s_cols, 1)

                chunk_loop(dve, chunk, NPC, st, 2 * TPC + 2)
                evacuate(NPC - 2, 0, NPC // 2 - 1)
                evacuate(NPC - 1, 1, NPC // 2 - 1)

            @block.scalar
            def _(act):
                def copy_state(i, par, use):
                    act.wait_ge(s_tr, TPC * (i + 1))
                    need(act, s_hst[par], 16 * use)
                    need(act, s_pm, i - 1)
                    nc.scalar.activation(hT[par][:].rearrange("f (p t) -> f t p", t=TPC), psT[par][:], ACT.Copy
                                         ).then_inc(s_hT, 1)

                def chunk(i, par, use):
                    act.wait_ge(s_stat, i + 1)
                    nc.scalar.activation(root[:, par], mv[:, par, :, 1], ACT.Sqrt, bias=epsc[:, 0:1]
                                         ).then_inc(s_root, 1)
                    if not isinstance(i, int) or i >= 1:
                        copy_state(i - 1, *behind(par, use, 1))
                    act.wait_ge(s_cols, i + 1)
                    need(act, s_tr, TPC * (i - 1))
                    for t in range(TPC):
                        nc.scalar.activation(rb[par][:, t, :], xb[par][:, t, 0:D], ACT.Relu,
                                             bias=cols[:, par, 1, t:t + 1], scale=cols[:, par, 0, t:t + 1]
                                             ).then_inc(s_relu, 1)

                chunk_loop(act, chunk, NPC)
                copy_state(NPC - 1, 1, NPC // 2 - 1)

            @block.tensor
            def _(pe):
                pe.wait_ge(s_srt, 1)
                nc.tensor.matmul(psR[:], row0[:], rankf[:], start=True, stop=True).then_inc(s_srt, 1)
                pe.wait_ge(s_w, 16 * 7)

                def messages(i, par, use):
                    pe.wait_ge(s_hT, i + 1)
                    need(pe, s_me, i - 1)
                    for t in range(TPC):
                        ins = nc.tensor.matmul(psM[par][:, t, :], hT[par][:, t:CW:TPC], wmsg[:], start=True, stop=True)
                    ins.then_inc(s_pm, 1)

                def chunk(i, par, use):
                    pe.wait_ge(s_relu, TPC * (i + 1))
                    need(pe, s_hT, i - 1)
                    for t in range(TPC):
                        nc.tensor.transpose(psT[par][:, t, :], rb[par][:, t, :], ident[:]).then_inc(s_tr, 1)
                    if not isinstance(i, int) or i >= 1:
                        messages(i - 1, *behind(par, use, 1))

                chunk_loop(pe, chunk, NPC)
                messages(NPC - 1, 1, NPC // 2 - 1)

        HALF = NPC // 2
        TQ = EC // HALF
        s_hin = [sem("r_hin0"), sem("r_hin1")]
        s_g = [sem("r_g0"), sem("r_g1")]
        s_ib = sem("r_ib")
        s_clr = sem("r_clear")
        s_hn, s_pr, s_pz, s_pi = sem("r_hn"), sem("r_pr"), sem("r_pz"), sem("r_pi")
        s_r, s_z, s_n = sem("r_r"), sem("r_z"), sem("r_n")
        s_t1, s_t2 = sem("r_t1"), sem("r_t2")
        s_d1, s_d2, s_h = sem("r_d1"), sem("r_d2"), sem("r_h")
        s_sb, s_sel, s_ev = sem("r_sb"), sem("r_sel"), sem("r_ev")
        s_pm, s_me = sem("r_pm"), sem("r_me")
        s_x2 = [sem("r_x0"), sem("r_x1")]
        s_fin = [sem("r_fin0"), sem("r_fin1")]
        s_tk = sem("r_tick")
        c6 = ExitStack()
        with c6:
            hin = [sb(f"r_hin{i}", [P, CW], F32, c6) for i in range(2)]
            hnew = [sb(f"r_hnew{i}", [P, CW], F32, c6) for i in range(2)]
            rs = [sb(f"r_r{i}", [P, CW], F32, c6) for i in range(2)]
            zs = [sb(f"r_z{i}", [P, CW], F32, c6) for i in range(2)]
            ns = [sb(f"r_n{i}", [P, CW], F32, c6) for i in range(2)]
            ts = [sb(f"r_t{i}", [P, CW], F32, c6) for i in range(2)]
            dsb = sb("r_d", [P, CW], F32, c6)
            mb = [sb(f"r_m{i}", [P, TPC, D], F32, c6) for i in range(2)]
            G = [sb(f"r_G{i}", [P, TQ, D], F32, c6) for i in range(2)]
            ib = sb("r_ib", [P, 2, TQ], I32, c6)
            sel = sb("r_sel", [P, TQ, SW], F32, c6)
            zero = sb("r_zero", [P, CW], F32, c6)
            x2b = [sb(f"r_x2{i}", [P, TPC, IDW], F32, c6) for i in range(2)]
            psHN = [pb(f"r_psHN{i}", [P, CW], F32, c6) for i in range(2)]
            psR = pb("r_psR", [P, CW], F32, c6)
            psZ = pb("r_psZ", [P, CW], F32, c6)
            psI = pb("r_psI", [P, CW], F32, c6)
            psM = pb("r_psM", [P, TPC, D], F32, c6)
            psS = [pb(f"r_psS{i}", [P, 512], F32, c6) for i in range(2)]
            block = c6.enter_context(nc.Block())

            def steps(eng, step):
                def two(k):
                    step(2 * k, 0, 1, False)
                    step(2 * k + 1, 1, 0, False)

                engine_loop(eng, STEPS // 2, two)
                step(STEPS - 1, 0, 1, True)

            @block.sync
            def _(sp):
                def step(s, src_m, dst_m, last):
                    done = NPC * s

                    def load(c, par):
                        sp.dma_start(hin[par][:], htv[:, bass.ds(c, 1), :].rearrange("f c n -> f (c n)")
                                     ).then_inc(s_hin[par], 16)

                    def store_m(c, par):
                        sp.wait_ge(s_me, done + c + 2)
                        sp.dma_start(msgv[dst_m][bass.ds(c, 1)].rearrange("c p n -> (c p) n"),
                                     mb[par][:].rearrange("p t f -> p (t f)")).then_inc(s_mst[par], 16)

                    def load_x2(c, par, use):
                        need(sp, s_fin[par], 16 * TPC * use)
                        sp.dma_start(x2b[par][:], x2v[bass.ds(c, 1)].rearrange("c p t w -> (c p) t w")
                                     ).then_inc(s_x2[par], 16)

                    def chunk(c, par, use):
                        sp.wait_ge(s_h, done + c + 1)
                        if not last:
                            sp.dma_start(htv[:, bass.ds(c, 1), :].rearrange("f c n -> f (c n)"), hnew[par][:]
                                         ).then_inc(s_hst[par], 16)
                        if not isinstance(c, int) or c < NPC - 2:
                            load(c + 2, par)
                        if not isinstance(c, int) or c >= 1:
                            if not last:
                                store_m(c - 1, 1 - par)
                            elif not isinstance(c, int) or c < NPC - 1:
                                load_x2(c + 1, *behind(par, use, -1))

                    load(0, 0)
                    load(1, 1)
                    if last:
                        load_x2(0, 0, 0)
                        load_x2(1, 1, 0)
                    two_halves(sp, chunk, chunk, tail=2)
                    if not last:
                        store_m(NPC - 1, 1)

                steps(sp, step)
                for par in range(2):
                    sp.wait_ge(s_hst[par], 16 * HALF * STEPS)
                    sp.wait_ge(s_mst[par], 16 * HALF * STEPS)

            @block.gpsimd
            def _(pool):
                ids = [[x2b[par][:, t, D:D + 1].bitcast(I32) for t in range(TPC)] for par in range(2)]
                nc.gpsimd.memset(zero[:], 0.0).then_inc(s_clr, 1)
                pool.wait_ge(s_clr, 1)

                def step(s, src_m, dst_m, last):
                    for par in range(2):
                        pool.wait_ge(s_mst[par], 16 * HALF * (s + 1))

                    def scatter(c, par):
                        pool.wait_ge(s_me, NPC * s + c + 2)
                        pool.sem_inc(s_tk, 1)
                        for t in range(TPC):
                            pool.indirect_dma_start(out, bass.IndirectOffsetOnAxis(ap=ids[par][t], axis=0),
                                                    mb[par][:, t, :], None, bounds_check=N - 1, oob_is_err=False
                                                    ).then_inc(s_fin[par], 16)

                    def gather(c, par):
                        pool.wait_ge(s_sel, TQ * (HALF * s + c + 1))
                        pool.sem_inc(s_tk, 1)
                        nc.gpsimd.tensor_copy(ib[:, par], srow[:, bass.ds(TQ * c, TQ)]).then_inc(s_ib, 1)
                        pool.wait_ge(s_ib, HALF * s + c + 1)
                        pool.sem_inc(s_tk, 1)
                        for q in range(TQ):
                            pool.indirect_dma_start(G[par][:, q, :], None, msg_tab[src_m],
                                                    bass.IndirectOffsetOnAxis(ap=ib[:, par, q:q + 1], axis=0)
                                                    ).then_inc(s_g[par], 16)

                    def clear(c):
                        pool.wait_ge(s_pi, HALF * s + c - HALF + 1)
                        pool.sem_inc(s_tk, 1)
                        nc.gpsimd.tensor_copy(agg[:, bass.ds(CW * (c - HALF), CW)], zero[:]).then_inc(s_clr, 1)

                    def first(c, par, use):
                        gather(c, par)
                        if last and not (isinstance(c, int) and c == 0):
                            scatter(c - 1, 1 - par)

                    def second(c, par, use):
                        if last:
                            scatter(c - 1, 1 - par)
                        else:
                            clear(c)

                    two_halves(pool, first, second)
                    if last:
                        scatter(NPC - 1, 1)

                steps(pool, step)
                for par in range(2):
                    pool.wait_ge(s_fin[par], 16 * TPC * HALF)

            @block.tensor
            def _(pe):
                def step(s, src_m, dst_m, last):
                    done = NPC * s

                    def finish(c, par):
                        pe.wait_ge(s_h, done + c + 1)
                        pe.wait_ge(s_me, done + c + 1)
                        for t in range(TPC):
                            if last:
                                ins = nc.tensor.transpose(psM[:, t, :], hnew[par][:, t:CW:TPC], ident[:])
                            else:
                                ins = nc.tensor.matmul(psM[:, t, :], hnew[par][:, t:CW:TPC], wmsg[:],
                                                       start=True, stop=True)
                        ins.then_inc(s_pm, 1)

                    def gates(c, par, use, edges):
                        pe.wait_ge(s_hin[par], 16 * (HALF * s + use + 1))
                        pe.wait_ge(s_t1, done + c + 1)
                        nc.tensor.matmul(psHN[par][:], whh[:, 2 * D:3 * D], hin[par][:], start=True, stop=True
                                         ).then_inc(s_hn, 1)
                        for g, ps, free, sig in ((0, psR, s_r, s_pr), (1, psZ, s_z, s_pz)):
                            pe.wait_ge(free, done + c + 1)
                            ins = nc.tensor.matmul(ps[:], whh[:, g * D:(g + 1) * D], hin[par][:], start=True,
                                                   stop=not edges)
                            if edges:
                                ins = nc.tensor.matmul(ps[:], wih[:, g * D:(g + 1) * D],
                                                       agg[:, bass.ds(CW * (c - HALF), CW)], start=False, stop=True)
                            ins.then_inc(sig, 1)
                        if edges:
                            pe.wait_ge(s_t2, HALF * s + c - HALF + 1)
                            nc.tensor.matmul(psI[:], wih[:, 2 * D:3 * D], agg[:, bass.ds(CW * (c - HALF), CW)],
                                             start=True, stop=True).then_inc(s_pi, 1)

                    def tiles(c, par, use):
                        pe.wait_ge(s_g[par], 16 * TQ * ((25 - par) * s + use + 1))
                        for q in range(TQ):
                            j = TQ * (HALF * s + c) + q
                            pe.wait_ge(s_sb, j + 1)
                            pe.wait_ge(s_ev, j + TQ - 1)
                            nc.tensor.matmul(psS[q % 2][:, 0:SW], G[par][:, q, :], sel[:, q, :],
                                             start=True, stop=True).then_inc(s_sel, 1)

                    def first(c, par, use):
                        gates(c, par, use, False)
                        tiles(c, par, use)
                        if not (isinstance(c, int) and c == 0):
                            finish(c - 1, 1 - par)

                    def second(c, par, use):
                        if isinstance(c, int) and c == HALF:
                            pe.wait_ge(s_ev, EC * (s + 1) + TQ)
                        gates(c, par, use, True)
                        finish(c - 1, 1 - par)

                    two_halves(pe, first, second)
                    finish(NPC - 1, 1)

                steps(pe, step)

            @block.scalar
            def _(act):
                act.sem_inc(s_r, 1)
                act.sem_inc(s_z, 1)

                def step(s, src_m, dst_m, last):
                    done = NPC * s

                    def chunk(c, par, edges):
                        act.wait_ge(s_pr, done + c + 1)
                        nc.scalar.activation(rs[par][:], psR[:], ACT.Sigmoid, bias=brz[:, 0:1]).then_inc(s_r, 1)
                        act.wait_ge(s_pz, done + c + 1)
                        nc.scalar.activation(zs[par][:], psZ[:], ACT.Sigmoid, bias=brz[:, 1:2]).then_inc(s_z, 1)
                        if edges:
                            act.wait_ge(s_t2, HALF * s + c - HALF + 2)
                        else:
                            act.wait_ge(s_t1, done + c + 3)
                        nc.scalar.activation(ns[par][:], ts[par][:], ACT.Tanh, bias=bih[:, 2:3]).then_inc(s_n, 1)

                    two_halves(act, lambda c, par, use: chunk(c, par, False), lambda c, par, use: chunk(c, par, True))

                steps(act, step)

            @block.vector
            def _(dve):
                dve.sem_inc(s_t1, 2)
                dve.sem_inc(s_t2, 1)
                dve.sem_inc(s_d2, 1)
                dve.sem_inc(s_me, 1)
                dve.sem_inc(s_sel, 2 * TQ)
                dve.sem_inc(s_ev, TQ)
                dve.wait_ge(s_clr, 1)

                def step(s, src_m, dst_m, last):
                    done = NPC * s
                    chunks = HALF * s

                    def select(c):
                        for q in range(TQ):
                            j = TQ * (chunks + c) + q
                            dve.wait_ge(s_sel, j + 2 * TQ - 3)
                            nc.vector.tensor_scalar(sel[:, q, :], iota_w[:, 0:SW], lrank[:, bass.ds(TQ * c + q, 1)],
                                                    None, ALU.is_equal).then_inc(s_sb, 1)

                    def add(c):
                        for q in range(TQ):
                            j = TQ * (chunks + c) + q
                            at = dve.value_load(base[0:1, bass.ds(TQ * c + q, 1)], min_val=0, max_val=E)
                            dve.wait_ge(s_sel, j + 2 * TQ + 1)
                            dve.wait_ge(s_ev, j + TQ)
                            nc.vector.tensor_tensor(agg[:, bass.ds(at, SW)], psS[q % 2][:, 0:SW],
                                                    agg[:, bass.ds(at, SW)], ALU.add).then_inc(s_ev, 1)

                    def evacuate(c, par, use):
                        dve.wait_ge(s_pm, done + c + 1)
                        if last:
                            dve.wait_ge(s_x2[par], 16 * (use + 1))
                            need(dve, s_fin[par], 16 * TPC * use)
                            other = x2b[par][:, :, 0:D]
                        else:
                            dve.wait_ge(s_mst[par], 16 * (HALF * (s + 1) + use))
                            other = bmsg[:].unsqueeze(1).to_broadcast([P, TPC, D])
                        nc.vector.tensor_tensor(mb[par][:], psM[:], other, ALU.add).then_inc(s_me, 1)

                    def hidden(c, par, edges):
                        dve.wait_ge(s_hn, done + c + 1)
                        dve.wait_ge(s_r, done + c + 2)
                        nc.vector.scalar_tensor_tensor(ts[par][:], psHN[par][:], bhh[:, 2:3], rs[par][:],
                                                       ALU.add, ALU.mult).then_inc(s_t1, 1)
                        if edges:
                            dve.wait_ge(s_pi, chunks + c - HALF + 1)
                            dve.wait_ge(s_t1, done + c + 3)
                            nc.vector.tensor_tensor(ts[par][:], ts[par][:], psI[:], ALU.add).then_inc(s_t2, 1)

                    def update(c, par, use):
                        dve.wait_ge(s_n, done + c + 1)
                        dve.wait_ge(s_d2, done + c + 1)
                        nc.vector.tensor_tensor(dsb[:], hin[par][:], ns[par][:], ALU.subtract).then_inc(s_d1, 1)
                        dve.wait_ge(s_z, done + c + 2)
                        dve.wait_ge(s_d1, done + c + 1)
                        nc.vector.tensor_tensor(dsb[:], dsb[:], zs[par][:], ALU.mult).then_inc(s_d2, 1)
                        dve.wait_ge(s_d2, done + c + 2)
                        if not last:
                            dve.wait_ge(s_hst[par], 16 * (HALF * (s + 1) + use))
                        nc.vector.tensor_tensor(hnew[par][:], ns[par][:], dsb[:], ALU.add).then_inc(s_h, 1)

                    def first(c, par, use):
                        if isinstance(c, int) and c == 0:
                            dve.wait_ge(s_clr, chunks + 1)
                        select(c)
                        hidden(c, par, False)
                        add(c)
                        if not (isinstance(c, int) and c == 0):
                            evacuate(c - 1, *behind(par, use, 1))
                        update(c, par, use)

                    def second(c, par, use):
                        hidden(c, par, True)
                        evacuate(c - 1, *behind(par, use, 1))
                        update(c, par, use)

                    if last:
                        for par in range(2):
                            dve.wait_ge(s_mst[par], 16 * HALF * STEPS)
                            dve.wait_ge(s_hst[par], 16 * HALF * STEPS)
                    two_halves(dve, first, second)
                    evacuate(NPC - 1, 1, HALF - 1)

                steps(dve, step)


def normalise(nc, st, h, o, a, scale, shift):
    st.mark(nc.vector.scalar_tensor_tensor(o, h[:], a[:, 0:1], o, ALU.mult, ALU.add))
    st.wait()
    st.mark(nc.vector.tensor_tensor(o, o, scale, ALU.mult))
    st.wait()
    st.mark(nc.vector.tensor_tensor(o, o, shift, ALU.add))
    st.wait()
    st.mark(nc.vector.tensor_tensor(o, o, h[:], ALU.add))


_CONV = ["W", "b", "cw", "cb", "a", "g", "be", "blank"]
_GRU = ["W_msg", "b_msg", "W_ih", "W_hh", "b_ih", "b_hh"]


def kernel(**inputs):
    import numpy as _np
    import concourse.bacc as _bacc
    from concourse import mybir as _mybir
    from concourse.bass_utils import run_bass_kernel_spmd as _run

    nc = _bacc.Bacc("TRN2", target_bir_lowering=False, num_devices=1)
    arrays = {}

    def given(name, transposed=False):
        a = _np.asarray(inputs[name])
        a = _np.ascontiguousarray(a.T if transposed else a)
        arrays[f"in_{name}_dram"] = a
        return nc.dram_tensor(f"in_{name}_dram", a.shape, _mybir.dt.from_np(a.dtype), kind="ExternalInput").ap()

    x, src, dst = given("x"), given("src"), given("dst")
    conv = [[given(f"L0_gnn_{p}{i}", p == "W") for p in _CONV] for i in range(2)]
    gru = [given(f"L1_gnn_{p}", p.startswith("W_")) for p in _GRU]
    out = nc.dram_tensor("out_0_dram", (N, D), F32, kind="ExternalOutput").ap()
    build(nc, x, src, dst, conv, gru, out)
    r = _run(nc, [arrays], core_ids=[0])
    return r.results[0]["out_0_dram"]
```

```python
from contextlib import ExitStack

import concourse.bass as bass
from concourse import mybir

F32 = mybir.dt.float32
BF16 = mybir.dt.bfloat16
I32 = mybir.dt.int32
ALU = mybir.AluOpType
ACT = mybir.ActivationFunctionType
AX = mybir.AxisListType


P = 128
N, D, E = 50000, 128, 25000
LO, HI = 128, 392
NPAD = LO * HI
EC = 196
EPAD = P * EC
EREM = E - (P - 1) * EC
RT = 8
NCH = NPAD // (P * RT)
LASTP = (N - (NCH - 1) * P * RT) // RT
EQ = EC // NCH
JG = 14
NG = EC // JG
CW = 512
NACT = EPAD // CW
SW = P + 1
IDW = D + 4
LNEPS = 1e-5
BNEPS = 1e-5
STEPS = 5
FAR = 1 << 20


class Steps:

    def __init__(self, eng, sem):
        self.eng, self.sem, self.base, self.n = eng, sem, 0, 0

    def mark(self, ins):
        ins.then_inc(self.sem, 1)
        self.n += 1

    def here(self):
        return self.base + self.n

    def wait(self):
        self.eng.wait_ge(self.sem, self.here())


def engine_loop(eng, trips, body, steps=None, per=0):
    if steps is None:
        with eng.Fori(0, trips) as k:
            body(k)
        return
    base, n = steps.base, steps.n
    with eng.Fori(0, trips) as k:
        steps.base, steps.n = base + n + k * per, 0
        body(k)
        assert steps.n == per, (steps.n, per)
    steps.base, steps.n = base, n + trips * per


def chunk_loop(eng, body, n=NCH, steps=None, per=0, peel=2):
    for i in range(peel):
        body(i, i % 2, i // 2)

    def both(k):
        body(2 * k + peel, 0, k + peel // 2)
        body(2 * k + peel + 1, 1, k + peel // 2)

    engine_loop(eng, (n - peel) // 2, both, steps, 2 * per)
    if n % 2:
        body(n - 1, 0, n // 2)


def two_halves(eng, first, second, half=EPAD // CW, tail=0):
    for c in range(3):
        first(c, c % 2, c // 2)

    def a(k):
        first(2 * k + 3, 1, k + 1)
        first(2 * k + 4, 0, k + 2)

    engine_loop(eng, half // 2 - 1, a)
    second(half, 1, half // 2)

    def b(k):
        second(2 * k + half + 1, 0, k + (half + 1) // 2)
        second(2 * k + half + 2, 1, k + (half + 1) // 2)

    engine_loop(eng, (half - tail) // 2, b)
    for c in range(2 * half - tail, 2 * half):
        second(c, c % 2, c // 2)


def behind(par, use, lag):
    return (par - lag) % 2, use - (lag + 1 - par) // 2


def need(eng, sem, value):
    if not (isinstance(value, int) and value <= 0):
        eng.wait_ge(sem, value)


def build(nc, x, src, dst, conv, gru, out):
    ctx = ExitStack()

    def sb(name, shape, dt=F32, c=ctx):
        return c.enter_context(nc.sbuf_tensor(name, shape, dt))

    def pb(name, shape, dt=F32, c=ctx):
        return c.enter_context(nc.psum_tensor(name, shape, dt))

    def sem(name):
        return ctx.enter_context(nc.semaphore(name))

    def dram(name, shape, dt=F32):
        return nc.dram_tensor(name, shape, dt).ap()

    h_tab = [dram("h0_tab", (NPAD, D)), dram("h1_tab", (NPAD, D))]
    o_tab = [dram("o0_tab", (NPAD, D)), dram("o1_tab", (NPAD, D))]
    x2_tab = dram("x2_tab", (NPAD, IDW))
    ht_tab = dram("ht_tab", (D, NPAD))
    msg_tab = [dram("msg0_tab", (NPAD, D)), dram("msg1_tab", (NPAD, D))]
    node_tab = dram("node_tab", (NPAD, 2), I32)
    sort_tab = dram("sort_tab", (EPAD, 2), I32)

    with ctx:
        ident = sb("ident", [P, P])
        identb = sb("identb", [P, P], BF16)
        ones = sb("ones", [P, P])
        ones_last = sb("ones_last", [P, P])
        later = sb("later", [P, P])
        row0 = sb("row0", [P, P])
        iota_p = sb("iota_p", [P, 1])
        iota_w = sb("iota_w", [P, HI])
        epsc = sb("epsc", [P, 1])
        edge_src = sb("edge_src", [P, EC + 3], I32)
        gat_src = sb("gat_src", [P, EC + 3], I32)
        edge_dst = sb("edge_dst", [P, EC + 4], I32)
        same1 = sb("same1", [P, EC + 2], I32)
        same2 = sb("same2", [P, EC], I32)
        put_idx = sb("put_idx", [P, EC], I32)
        src_at = sb("src_at", [P, EC], I32)
        dst_at = sb("dst_at", [P, EC], I32)
        occ = sb("occ", [P, EC])
        look = sb("look", [P, EC, 2], I32)
        pair = sb("pair", [P, EC, 2], I32)
        sort_at = sb("sort_at", [P, EC], I32)
        node_pos = sb("node_pos", [P, HI], I32)

        s_ld = sem("s1_load")
        s_ms = sem("s1_memset")
        s_io = sem("s1_iota")
        s_dv = sem("s1_dve")
        s_pe = sem("s1_pe")
        blank_o = [sb("blank_o0", [P, D]), sb("blank_o1", [P, D])]
        blank_p = [sb("blank_p0", [P, D]), sb("blank_p1", [P, D])]
        cwb = [sb(f"cwb{i}", [P, 4]) for i in range(2)]
        cbb = [sb(f"cbb{i}", [P, 1]) for i in range(2)]
        ab = [sb(f"ab{i}", [P, 1]) for i in range(2)]
        gb = [sb(f"gb{i}", [P, D]) for i in range(2)]
        beb = [sb(f"beb{i}", [P, D]) for i in range(2)]
        filled = [sb("o_blank0", [P, RT * D]), sb("o_blank1", [P, RT * D])]
        c1 = ExitStack()
        with c1:
            iw_i = sb("iw_i", [P, HI], I32, c1)
            ip_i = sb("ip_i", [P, 1], I32, c1)
            wt = [sb(f"wt{i}", [P, D], F32, c1) for i in range(2)]
            bb = [sb(f"bb{i}", [P, D], F32, c1) for i in range(2)]
            blc = [sb(f"blc{i}", [P, 1], F32, c1) for i in range(2)]
            blw = [sb(f"blw{i}", [P, P], F32, c1) for i in range(2)]
            dstf = sb("dstf", [P, EC + 4], F32, c1)
            tmpf = sb("tmpf", [P, EC], F32, c1)
            tmpg = sb("tmpg", [P, EC], F32, c1)
            pbl = [pb(f"pbl{i}", [P, D], F32, c1) for i in range(2)]
            block = c1.enter_context(nc.Block())
            loads = []

            @block.sync
            def _(sp):
                sp.wait_ge(s_ms, 2)
                m = (P - 1) * EC
                for t, s, o in ((edge_src, src, 0), (edge_dst, dst, 1)):
                    loads.append(sp.dma_start(t[0:P - 1, o:o + EC], s[0:m].rearrange("(p j) -> p j", j=EC)))
                    loads.append(sp.dma_start(t[P - 1:P, o:o + EREM], s[m:E].rearrange("(p j) -> p j", p=1)))
                    loads.append(sp.dma_start(t[0:P - 2, o + EC:o + EC + 3],
                                              s[EC:m].rearrange("(p j) -> p j", j=EC)[:, 0:3]))
                    loads.append(sp.dma_start(t[P - 2:P - 1, o + EC:o + EC + 3],
                                              s[m:m + 3].rearrange("(p j) -> p j", p=1)))
                loads.append(sp.dma_start(edge_dst[1:P, 0:1], dst[0:m].rearrange("(p j) -> p j", j=EC)[:, EC - 1:EC],
                                          allow_slow_non_contiguous=True))
                for i in range(2):
                    W, b, cw, cb, a, g, be, bl = conv[i]
                    loads.append(sp.dma_start(wt[i][:], W))
                    loads.append(sp.dma_start(blc[i][:], bl.rearrange("(p o) -> p o", o=1)))
                    for t, v in ((bb[i], b), (cwb[i], cw), (cbb[i], cb), (ab[i], a), (gb[i], g), (beb[i], be)):
                        loads.append(sp.dma_start(t[:], v.partition_broadcast(P)))
                for ins in loads:
                    ins.then_inc(s_ld, 16)

            NLOAD = 9 + 16

            @block.gpsimd
            def _(pool):
                nc.gpsimd.memset(edge_src[:], NPAD).then_inc(s_ms, 1)
                nc.gpsimd.memset(edge_dst[:], -1).then_inc(s_ms, 1)
                nc.gpsimd.iota(iw_i[:], [[1, HI]], base=0, channel_multiplier=0).then_inc(s_io, 1)
                nc.gpsimd.iota(ip_i[:], [[1, 1]], base=0, channel_multiplier=1).then_inc(s_io, 1)

            @block.vector
            def _(dve):
                st = Steps(dve, s_dv)
                dve.wait_ge(s_io, 2)
                st.mark(nc.vector.memset(ones[:], 1.0))
                st.mark(nc.vector.memset(epsc[:], LNEPS))
                st.mark(nc.vector.tensor_copy(iota_w[:], iw_i[:]))
                st.mark(nc.vector.tensor_copy(iota_p[:], ip_i[:]))
                st.wait()
                st.mark(nc.vector.tensor_scalar(ident[:], iota_w[:, 0:P], iota_p[:, 0:1], None, ALU.is_equal))
                st.mark(nc.vector.tensor_scalar(identb[:], iota_w[:, 0:P], iota_p[:, 0:1], None, ALU.is_equal))
                st.mark(nc.vector.tensor_scalar(later[:], iota_w[:, 0:P], iota_p[:, 0:1], None, ALU.is_gt))
                st.mark(nc.vector.tensor_scalar(row0[:], ones[:], iota_p[:, 0:1], 0.0, ALU.mult, ALU.is_equal))
                st.mark(nc.vector.tensor_scalar(ones_last[:], ones[:], iota_p[:, 0:1], float(LASTP),
                                                ALU.mult, ALU.is_lt))
                dve.wait_ge(s_ld, 16 * NLOAD)
                for i in range(2):
                    st.mark(nc.vector.tensor_scalar(blw[i][:], ones[:], blc[i][:, 0:1], None, ALU.mult))
                st.mark(nc.vector.tensor_copy(dstf[:], edge_dst[:]))
                for at, e in ((src_at, edge_src[:, 0:EC]), (dst_at, edge_dst[:, 1:EC + 1])):
                    st.wait()
                    st.mark(nc.vector.tensor_scalar(at[:], e, LO - 1, None, ALU.bitwise_and))
                    st.mark(nc.vector.tensor_scalar(sort_at[:], e, 7, None, ALU.logical_shift_right))
                    st.wait()
                    st.mark(nc.vector.tensor_copy(tmpf[:], at[:]))
                    st.mark(nc.vector.tensor_copy(tmpg[:], sort_at[:]))
                    st.wait()
                    st.mark(nc.vector.tensor_scalar(tmpf[:], tmpf[:], float(HI), None, ALU.mult))
                    st.wait()
                    st.mark(nc.vector.tensor_tensor(tmpf[:], tmpf[:], tmpg[:], ALU.add))
                    st.wait()
                    st.mark(nc.vector.tensor_scalar(at[:], tmpf[:], float(NPAD - 1), None, ALU.min))
                st.wait()
                st.mark(nc.vector.tensor_scalar(gat_src[:], edge_src[:], float(N), None, ALU.min))
                st.mark(nc.vector.tensor_tensor(same1[:], dstf[:, 1:EC + 3], dstf[:, 2:EC + 4], ALU.is_equal))
                st.mark(nc.vector.tensor_tensor(same2[:], dstf[:, 1:EC + 1], dstf[:, 3:EC + 3], ALU.is_equal))
                st.mark(nc.vector.tensor_tensor(tmpf[:], dstf[:, 1:EC + 1], dstf[:, 0:EC], ALU.is_equal))
                st.mark(nc.vector.tensor_scalar(tmpg[:], dstf[:, 1:EC + 1], 0.0, None, ALU.is_lt))
                st.wait()
                st.mark(nc.vector.tensor_tensor(tmpf[:], tmpf[:], tmpg[:], ALU.add))
                st.wait()
                st.mark(nc.vector.scalar_tensor_tensor(put_idx[:], tmpf[:], float(FAR), dstf[:, 1:EC + 1],
                                                       ALU.mult, ALU.add))
                dve.wait_ge(s_pe, 2)
                for i in range(2):
                    st.mark(nc.vector.tensor_tensor(blank_p[i][:], pbl[i][:], bb[i][:], ALU.add))
                st.wait()
                for i in range(2):
                    st.mark(nc.vector.tensor_scalar(blank_o[i][:], blank_p[i][:], cwb[i][:, 0:1], cbb[i][:, 0:1],
                                                    ALU.mult, ALU.add))
                for m in range(1, 4):
                    st.wait()
                    for i in range(2):
                        st.mark(nc.vector.scalar_tensor_tensor(blank_o[i][:], blank_p[i][:], cwb[i][:, m:m + 1],
                                                               blank_o[i][:], ALU.mult, ALU.add))
                st.wait()
                for i in range(2):
                    st.mark(nc.vector.tensor_copy(filled[i][:].rearrange("p (t f) -> p t f", f=D),
                                                  blank_o[i][:].unsqueeze(1).to_broadcast([P, RT, D])))
                st.wait()

            @block.tensor
            def _(pe):
                pe.wait_ge(s_dv, 11)
                for i in range(2):
                    nc.tensor.matmul(pbl[i][:], blw[i][:], wt[i][:], start=True, stop=True).then_inc(s_pe, 1)

        s_fill = sem("s2_fill")
        s_xin = [sem("s2_x0"), sem("s2_x1")]
        s_xfree = [sem("s2_xf0"), sem("s2_xf1")]
        s_pad = sem("s2_pad")
        s_stat = sem("s2_stat")
        s_root = sem("s2_root")
        s_cols = sem("s2_cols")
        s_rows = sem("s2_rows")
        s_hout = [sem("s2_h0"), sem("s2_h1")]
        s_dv2 = sem("s2_dve")
        s_tick = sem("s2_tick")
        s_all = sem("s2_allsrc")
        s_dig = sem("s2_digits")
        s_stage = sem("s2_stage")
        s_low = sem("s2_low")
        s_hot = sem("s2_hot")
        s_hotT = sem("s2_hotT")
        s_hotc = sem("s2_hotc")
        s_cnt = sem("s2_cnt")
        s_run = sem("s2_run")
        s_look = sem("s2_look")
        s_red = sem("s2_red")
        cnt_lo = sb("cnt_lo", [P, EQ, HI])
        c2 = ExitStack()
        with c2:
            xb = [sb(f"xb{i}", [P, RT, D], F32, c2) for i in range(2)]
            hb = [sb(f"hb{i}", [P, RT, D], F32, c2) for i in range(2)]
            stats = sb("stats", [P, RT, 6], F32, c2)
            mv = sb("mv", [P, 2, RT, 2], F32, c2)
            root = sb("root", [P, 2, RT], F32, c2)
            cols = sb("ln_cols", [P, 2, 2, RT], F32, c2)
            allsrc = sb("allsrc", [P, EPAD], I32, c2)
            srcf = sb("srcf", [P, EC], F32, c2)
            lof = sb("lof", [P, EC], F32, c2)
            hif = sb("hif", [P, EC], F32, c2)
            tmpi = sb("tmpi", [P, EC], I32, c2)
            hot_lo = sb("hot_lo", [P, 2, EQ, P], BF16, c2)
            hot_hi = sb("hot_hi", [P, 2, EQ, HI], BF16, c2)
            dig = sb("dig", [P, 2, EQ], F32, c2)
            hotT = sb("hotT", [P, 2, P], F32, c2)
            earlier = sb("earlier", [P, P], F32, c2)
            within = sb("within", [P, EC], F32, c2)
            before = sb("before", [P, EC], F32, c2)
            sums = sb("sums", [P, 2, EQ], F32, c2)
            junk = sb("junk", [P, 2, P], F32, c2)
            junk2 = sb("junk2", [P, 2, HI], F32, c2)
            psT = pb("psT", [P, P], BF16, c2)
            psC = pb("psC", [P, HI], F32, c2)
            psL = [pb(f"psL{i}", [P, HI], F32, c2) for i in range(EQ)]
            block = c2.enter_context(nc.Block())
            DV = 2 * RT + 4 + EQ

            @block.sync
            def _(sp):
                sp.wait_ge(s_pad, 1)
                sp.dma_start(allsrc[:, 0:E], src.partition_broadcast(P)).then_inc(s_all, 16)
                xf = x[0:(NCH - 1) * P * RT, :].rearrange("(c p t) f -> c p t f", p=P, t=RT)
                of = [o_tab[i].rearrange("(c p t) f -> c p (t f)", p=P, t=RT) for i in range(2)]

                def load(i, par, use):
                    sp.wait_ge(s_xfree[par], use + 1)
                    sp.dma_start(xb[par][:], xf[bass.ds(i, 1)].rearrange("c p t f -> (c p) t f")
                                 ).then_inc(s_xin[par], 16)
                    for q in range(2):
                        sp.dma_start(of[q][bass.ds(i, 1)].rearrange("c p n -> (c p) n"), filled[q][:]
                                     ).then_inc(s_fill, 16)

                chunk_loop(sp, load, NCH - 1)
                sp.wait_ge(s_xfree[0], NCH // 2 + 1)
                sp.wait_ge(s_pad, 2)
                sp.dma_start(xb[0][0:LASTP], x[(NCH - 1) * P * RT:N, :].rearrange("(p t) f -> p t f", t=RT)
                             ).then_inc(s_xin[0], 16)
                for q in range(2):
                    sp.dma_start(of[q][NCH - 1], filled[q][:]).then_inc(s_fill, 16)
                sp.wait_ge(s_fill, 16 * 2 * NCH)

            @block.gpsimd
            def _(pool):
                nc.gpsimd.memset(allsrc[:, E:EPAD], NPAD).then_inc(s_pad, 1)
                pool.wait_ge(s_dig, 1)
                pool.sem_inc(s_tick, 1)

                def chunk(i, par, use):
                    pool.wait_ge(s_red, EQ * i)
                    pool.sem_inc(s_tick, 1)
                    nc.gpsimd.tensor_copy(dig[:, par, :], hif[:, bass.ds(EQ * i, EQ)]).then_inc(s_stage, 1)
                    pool.wait_ge(s_stage, i + 1)
                    pool.sem_inc(s_tick, 1)
                    for q in range(EQ):
                        nc.gpsimd.tensor_scalar(hot_hi[:, par, q, :], iota_w[:], dig[:, par, q:q + 1], None,
                                                ALU.is_equal).then_inc(s_hot, 1)

                chunk_loop(pool, chunk, NCH - 1)
                pool.wait_ge(s_hot, EC - EQ)
                pool.wait_ge(s_xfree[0], NCH // 2 + 1)
                nc.gpsimd.memset(xb[0][96:P], 0.0).then_inc(s_pad, 1)
                pool.wait_ge(s_pad, 2)
                chunk(NCH - 1, 0, NCH // 2)

            @block.vector
            def _(dve):
                st = Steps(dve, s_dv2)
                ev = allsrc[:, :].rearrange("p (q j) -> p q j", j=EC)
                st.mark(nc.vector.memset(cnt_lo[:, 0], 0.0))
                st.mark(nc.vector.tensor_copy(srcf[:], edge_src[:, 0:EC]))
                st.mark(nc.vector.tensor_scalar(tmpi[:], edge_src[:, 0:EC], LO - 1, None, ALU.bitwise_and))
                st.wait()
                st.mark(nc.vector.tensor_copy(lof[:], tmpi[:]))
                st.wait()
                st.mark(nc.vector.tensor_scalar(tmpi[:], edge_src[:, 0:EC], 7, None, ALU.logical_shift_right))
                st.wait()
                st.mark(nc.vector.tensor_copy(hif[:], tmpi[:]))
                st.mark(nc.vector.tensor_scalar(earlier[:], iota_w[:, 0:P], iota_p[:, 0:1], None, ALU.is_lt))
                st.wait()
                dve.sem_inc(s_dig, 1)
                dve.sem_inc(s_run, 1)
                dve.sem_inc(s_red, EQ)
                dve.wait_ge(s_all, 16)

                def reduce(i, par):
                    for q in range(EQ):
                        dve.wait_ge(s_look, EQ * i + q + 1)
                        dve.wait_ge(s_red, EQ * i + q + EQ - 1)
                        nc.vector.tensor_tensor_reduce(
                            out=junk2[:, q % 2], in0=psL[q][:], in1=hot_hi[:, par, q, :], scale=1.0, scalar=0.0,
                            op0=ALU.mult, op1=ALU.add, accum_out=sums[:, 0, q:q + 1]).then_inc(s_red, 1)
                    dve.wait_ge(s_red, EQ * i + 2 * EQ)
                    st.mark(nc.vector.tensor_copy(before[:, bass.ds(EQ * i, EQ)], sums[:, 0, :]))

                def chunk(i, par, use):
                    need(dve, s_cnt, EQ * (i - 1))
                    for q in range(EQ):
                        nc.vector.tensor_scalar(hot_lo[:, par, q, :], iota_w[:, 0:P],
                                                lof[:, bass.ds(EQ * i + q, 1)], None, ALU.is_equal
                                                ).then_inc(s_low, 1)
                    dve.wait_ge(s_xin[par], 16 * (use + 1))
                    for t in range(RT):
                        st.mark(nc.vector.bn_stats(stats[:, t, :], xb[par][:, t, :]))
                    for q in range(EQ):
                        if q >= 2:
                            dve.wait_ge(s_dv2, st.here() - 1)
                        st.mark(nc.vector.scalar_tensor_tensor(
                            junk[:, q % 2], ev[:, :, bass.ds(EQ * i + q, 1)].rearrange("p q j -> p (q j)"),
                            srcf[:, bass.ds(EQ * i + q, 1)], earlier[:], ALU.is_equal, ALU.mult,
                            accum_out=sums[:, 1, q:q + 1]))
                    dve.wait_ge(s_dv2, st.here() - EQ)
                    dve.sem_inc(s_tick, 1)
                    for t in range(RT):
                        st.mark(nc.vector.bn_aggr(mv[:, par, t, :], stats[:, t, :]))
                    st.wait()
                    dve.sem_inc(s_stat, 1)
                    st.mark(nc.vector.tensor_copy(within[:, bass.ds(EQ * i, EQ)], sums[:, 1, :]))
                    if not isinstance(i, int) or i >= 2:
                        reduce(i - 2, par)
                    dve.wait_ge(s_root, i + 1)
                    st.mark(nc.vector.reciprocal(cols[:, par, 0, :], root[:, par, :]))
                    st.wait()
                    st.mark(nc.vector.scalar_tensor_tensor(cols[:, par, 1, :], mv[:, par, :, 0], -1.0,
                                                           cols[:, par, 0, :], ALU.mult, ALU.mult))
                    st.wait()
                    dve.sem_inc(s_cols, 1)

                chunk_loop(dve, chunk, NCH, st, DV)
                reduce(NCH - 2, 1)
                st.wait()
                reduce(NCH - 1, 0)
                st.wait()
                st.mark(nc.vector.tensor_tensor(occ[:], within[:], before[:], ALU.add))
                st.wait()

            @block.tensor
            def _(pe):
                def column(j, q, par, start=False):
                    pe.wait_ge(s_low, j + 1)
                    pe.wait_ge(s_hot, j + 1)
                    pe.wait_ge(s_hotc, j)
                    nc.tensor.transpose(psT[:], hot_lo[:, par, q, :], identb[:]).then_inc(s_hotT, 1)
                    pe.wait_ge(s_run, j + 1)
                    nc.tensor.matmul(psC[:], hot_lo[:, par, q, :], hot_hi[:, par, q, :], start=start, stop=True,
                                     skip_group_check=True).then_inc(s_cnt, 1)
                    if not start:
                        look_up(j - 1, (q - 1) % EQ)

                def look_up(j, q):
                    pe.wait_ge(s_hotc, j + 1)
                    pe.wait_ge(s_red, j + 1)
                    nc.tensor.matmul(psL[q][:], hotT[:, q % 2, :], cnt_lo[:, q, :], start=True, stop=True
                                     ).then_inc(s_look, 1)

                def chunk(i, par, use):
                    for q in range(EQ):
                        column(EQ * i + q, q, par, isinstance(i, int) and i == q == 0)

                chunk_loop(pe, chunk)
                look_up(EC - 1, EQ - 1)

            @block.scalar
            def _(act):
                for par in range(2):
                    act.sem_inc(s_xfree[par], 1)
                hf = h_tab[0].rearrange("(c p t) f -> c p (t f)", p=P, t=RT)

                def column(j, q):
                    act.wait_ge(s_hotT, j + 1)
                    nc.scalar.activation(hotT[:, q % 2, :], psT[:], ACT.Copy).then_inc(s_hotc, 1)
                    act.wait_ge(s_cnt, j + 1)
                    nc.scalar.activation(cnt_lo[:, (q + 1) % EQ, :], psC[:], ACT.Copy).then_inc(s_run, 1)

                def chunk(i, par, use):
                    act.wait_ge(s_stat, i + 1)
                    nc.scalar.activation(root[:, par], mv[:, par, :, 1], ACT.Sqrt, bias=epsc[:, 0:1]
                                         ).then_inc(s_root, 1)
                    if not isinstance(i, int) or i:
                        for q in range(EQ):
                            column(EQ * (i - 1) + q, q)
                    act.wait_ge(s_cols, i + 1)
                    need(act, s_hout[par], 16 * use)
                    for t in range(RT):
                        nc.scalar.activation(hb[par][:, t, :], xb[par][:, t, :], ACT.Relu,
                                             bias=cols[:, par, 1, t:t + 1], scale=cols[:, par, 0, t:t + 1]
                                             ).then_inc(s_rows, 1)
                    act.wait_ge(s_rows, RT * (i + 1))
                    act.sem_inc(s_xfree[par], 1)
                    act.dma_start(hf[bass.ds(i, 1)].rearrange("c p n -> (c p) n"),
                                  hb[par][:].rearrange("p t f -> p (t f)")).then_inc(s_hout[par], 16)

                chunk_loop(act, chunk)
                for q in range(EQ):
                    column(EQ * (NCH - 1) + q, q)
                act.wait_ge(s_hout[0], 16 * (NCH // 2 + 1))
                act.wait_ge(s_hout[1], 16 * (NCH // 2))

        s_dv3 = sem("s3_dve")
        s_pe3 = sem("s3_pe")
        s_out3 = sem("s3_out")
        node_look = sb("node_look", [P, HI, 2], I32)
        pay0 = sb("pay0", [P, EC, 2], I32)
        c3 = ExitStack()
        with c3:
            has = sb("has", [P, HI], F32, c3)
            ones_w = sb("ones_w", [P, HI], F32, c3)
            upto_hi = sb("upto_hi", [P, 2, HI], F32, c3)
            rank = sb("rank", [P, 2, HI], F32, c3)
            late = sb("late", [P, HI], F32, c3)
            ps = [pb(f"ps3_{i}", [P, HI], F32, c3) for i in range(4)]
            block = c3.enter_context(nc.Block())

            @block.vector
            def _(dve):
                st = Steps(dve, s_dv3)
                st.mark(nc.vector.tensor_scalar(has[:], cnt_lo[:, 0], 0.0, None, ALU.is_gt))
                st.mark(nc.vector.memset(ones_w[:], 1.0))
                st.mark(nc.vector.memset(pay0[:, :, 0], 0))
                st.mark(nc.vector.memset(pay0[:, :, 1], -FAR))
                st.mark(nc.vector.tensor_scalar(late[:], iota_w[:], float(LO), iota_p[:, 0:1], ALU.mult, ALU.add))
                st.wait()
                dve.wait_ge(s_pe3, 4)
                for q in range(2):
                    st.mark(nc.vector.tensor_tensor_scan(upto_hi[:, q], ones_w[:], ps[2 * q][:], 0.0,
                                                         ALU.mult, ALU.add))
                    st.wait()
                    st.mark(nc.vector.tensor_tensor(rank[:, q], upto_hi[:, q], ps[2 * q][:], ALU.subtract))
                    st.wait()
                    st.mark(nc.vector.tensor_tensor(rank[:, q], rank[:, q], ps[2 * q + 1][:], ALU.add))
                    st.wait()
                st.mark(nc.vector.tensor_tensor(late[:], late[:], rank[:, 1], ALU.subtract))
                st.wait()
                st.mark(nc.vector.tensor_scalar(late[:], late[:], upto_hi[:, 1, HI - 1:HI], None, ALU.add))
                st.wait()
                st.mark(nc.vector.tensor_tensor(rank[:, 1], rank[:, 1], late[:], ALU.subtract))
                st.wait()
                st.mark(nc.vector.tensor_tensor(rank[:, 1], rank[:, 1], has[:], ALU.mult))
                st.wait()
                st.mark(nc.vector.tensor_tensor(rank[:, 1], rank[:, 1], late[:], ALU.add))
                st.wait()
                st.mark(nc.vector.tensor_scalar(late[:], rank[:, 1], float(EPAD), float(-NPAD), ALU.is_ge, ALU.mult))
                st.wait()
                st.mark(nc.vector.tensor_scalar(rank[:, 1], rank[:, 1], float(EPAD), None, ALU.add))
                st.wait()
                st.mark(nc.vector.tensor_tensor(rank[:, 1], rank[:, 1], late[:], ALU.add))
                st.wait()
                st.mark(nc.vector.tensor_copy(node_look[:, :, 0], rank[:, 0]))
                st.mark(nc.vector.tensor_copy(node_look[:, :, 1], rank[:, 1]))
                st.mark(nc.vector.tensor_copy(node_pos[:], rank[:, 1]))
                st.wait()

            @block.tensor
            def _(pe):
                pe.wait_ge(s_dv3, 1)
                for q, m in enumerate((cnt_lo[:, 0], has[:])):
                    nc.tensor.matmul(ps[2 * q][:], ones[:], m, start=True, stop=True).then_inc(s_pe3, 1)
                    nc.tensor.matmul(ps[2 * q + 1][:], later[:], m, start=True, stop=True).then_inc(s_pe3, 1)

            @block.sync
            def _(sp):
                sp.wait_ge(s_dv3, 5)
                sp.dma_start(sort_tab.rearrange("(p j) w -> p j w", j=EC), pay0[:]).then_inc(s_out3, 16)
                sp.wait_ge(s_dv3, 22)
                sp.dma_start(node_tab.rearrange("(p j) w -> p j w", j=HI), node_look[:]).then_inc(s_out3, 16)
                sp.wait_ge(s_out3, 32)

        def pool_columns(pool, name, cbuf, table, idx, cols, scatter):
            s_cp = sem(name + "_cp")
            s_dma = [sem(name + "_d0"), sem(name + "_d1")]
            s_tk = sem(name + "_tk")
            ib = sb(name + "_ib", [P, 2, JG], I32, cbuf)
            rb = sb(name + "_rb", [P, 2, JG, 2], I32, cbuf)
            st = Steps(pool, s_cp)
            def group(i, par, use):
                pool.wait_ge(s_dma[par], 16 * JG * use)
                if not scatter:
                    take(i - 2, par)
                st.mark(nc.gpsimd.tensor_copy(ib[:, par], idx[:, bass.ds(JG * i, JG)]))
                if scatter:
                    st.mark(nc.gpsimd.tensor_copy(rb[:, par], cols[:, bass.ds(JG * i, JG), :]))
                st.wait()
                pool.sem_inc(s_tk, 1)
                issue(par)

            def take(i, par):
                st.mark(nc.gpsimd.tensor_copy(cols[:, bass.ds(JG * i, JG), :], rb[:, par]))
                st.wait()

            def issue(par):
                for q in range(JG):
                    if scatter:
                        pool.indirect_dma_start(table, bass.IndirectOffsetOnAxis(ap=ib[:, par, q:q + 1], axis=0),
                                                rb[:, par, q, :], None, bounds_check=EPAD - 1, oob_is_err=False
                                                ).then_inc(s_dma[par], 16)
                    else:
                        pool.indirect_dma_start(rb[:, par, q, :], None, table,
                                                bass.IndirectOffsetOnAxis(ap=ib[:, par, q:q + 1], axis=0)
                                                ).then_inc(s_dma[par], 16)

            for i in range(2):
                st.mark(nc.gpsimd.tensor_copy(ib[:, i], idx[:, JG * i:JG * (i + 1)]))
                if scatter:
                    st.mark(nc.gpsimd.tensor_copy(rb[:, i], cols[:, JG * i:JG * (i + 1), :]))
                st.wait()
                pool.sem_inc(s_tk, 1)
                issue(i)

            def both(k):
                group(2 * k + 2, 0, k + 1)
                group(2 * k + 3, 1, k + 1)

            engine_loop(pool, NG // 2 - 1, both, st, 4)
            for par in range(2):
                pool.wait_ge(s_dma[par], 16 * JG * (NG // 2))
                if not scatter:
                    take(NG - 2 + par, par)

        def convolve(layer):
            n = f"cv{layer}_"
            s_m = [sem(n + "m0"), sem(n + "m1")]
            s_m0 = sem(n + "m_first")
            s_done = sem(n + "m_done")
            s_halo = sem(n + "halo")
            s_fb = sem(n + "blank")
            s_fbf = sem(n + "blank_free")
            s_dv = sem(n + "dve")
            s_o = sem(n + "out")
            s_sc = [sem(n + "sc0"), sem(n + "sc1")]
            s_cp = sem(n + "cp")
            s_tk = sem(n + "tick")
            c = ExitStack()
            with c:
                M = [sb(f"{n}M{i}", [P, JG + 3, D], F32, c) for i in range(2)]
                S1 = [sb(f"{n}S{i}", [P, JG + 2, D], F32, c) for i in range(2)]
                L2 = [sb(f"{n}L{i}", [P, JG, D], F32, c) for i in range(2)]
                H2 = [sb(f"{n}H{i}", [P, JG, D], F32, c) for i in range(2)]
                low = sb(n + "low", [P, JG + 2, D], F32, c)
                high = sb(n + "high", [P, JG + 2, D], F32, c)
                A = sb(n + "A", [P, JG, D], F32, c)
                ob = [sb(f"{n}ob{i}", [P, JG, D], F32, c) for i in range(2)]
                ms1 = sb(n + "ms1", [P, 2, JG + 2], I32, c)
                ms2 = sb(n + "ms2", [P, 2, JG], I32, c)
                gi = sb(n + "gi", [P, 2, JG], I32, c)
                pi = sb(n + "pi", [P, 2, JG], I32, c)
                block = c.enter_context(nc.Block())

                @block.gpsimd
                def _(pool):
                    st = Steps(pool, s_cp)
                    for q in range(3):
                        pool.indirect_dma_start(M[0][:, q, :], None, h_tab[layer],
                                                bass.IndirectOffsetOnAxis(ap=gat_src[:, q:q + 1], axis=0)
                                                ).then_inc(s_m0, 16)

                    def gather(i, par):
                        pool.wait_ge(s_done, i + 1)
                        pool.wait_ge(s_halo, i + 1)
                        st.mark(nc.gpsimd.tensor_copy(gi[:, par], gat_src[:, bass.ds(JG * i + 3, JG)]))
                        st.wait()
                        pool.sem_inc(s_tk, 1)
                        for q in range(JG):
                            pool.indirect_dma_start(M[par][:, 3 + q, :], None, h_tab[layer],
                                                    bass.IndirectOffsetOnAxis(ap=gi[:, par, q:q + 1], axis=0)
                                                    ).then_inc(s_m[par], 16)

                    def scatter(i, par, use):
                        need(pool, s_sc[par], 16 * JG * use)
                        st.mark(nc.gpsimd.tensor_copy(pi[:, par], put_idx[:, bass.ds(JG * i, JG)]))
                        st.wait()
                        pool.wait_ge(s_o, i + 1)
                        pool.sem_inc(s_tk, 1)
                        for q in range(JG):
                            pool.indirect_dma_start(o_tab[layer],
                                                    bass.IndirectOffsetOnAxis(ap=pi[:, par, q:q + 1], axis=0),
                                                    ob[par][:, q, :], None, bounds_check=N - 1, oob_is_err=False
                                                    ).then_inc(s_sc[par], 16)

                    def group(i, par, use):
                        gather(i, par)
                        if not isinstance(i, int) or i:
                            scatter(i - 1, 1 - par, use + par - 1)

                    chunk_loop(pool, group, NG, st, 2)
                    scatter(NG - 1, 1, NG // 2 - 1)
                    for par in range(2):
                        pool.wait_ge(s_sc[par], 16 * JG * (NG // 2))

                @block.scalar
                def _(act):
                    act.sem_inc(s_halo, 2)
                    bl = blank_p[layer][:].unsqueeze(1)

                    def group(i, par, use):
                        act.wait_ge(s_fbf, i + 1)
                        nc.scalar.activation(S1[par][:], bl.to_broadcast([P, JG + 2, D]), ACT.Copy).then_inc(s_fb, 1)
                        nc.scalar.activation(L2[par][:], bl.to_broadcast([P, JG, D]), ACT.Copy).then_inc(s_fb, 1)
                        nc.scalar.activation(H2[par][:], bl.to_broadcast([P, JG, D]), ACT.Copy).then_inc(s_fb, 1)
                        nc.scalar.activation(ms1[:, par], same1[:, bass.ds(JG * i, JG + 2)], ACT.Copy
                                             ).then_inc(s_fb, 1)
                        nc.scalar.activation(ms2[:, par], same2[:, bass.ds(JG * i, JG)], ACT.Copy).then_inc(s_fb, 1)
                        if not isinstance(i, int) or i:
                            act.wait_ge(s_m[1 - par], 16 * JG * (use + (1 if par == 1 else 0)))
                            act.wait_ge(s_done, i + 1)
                            nc.scalar.activation(M[par][:, 0:3, :], M[1 - par][:, JG:JG + 3, :], ACT.Copy
                                                 ).then_inc(s_halo, 1)

                    chunk_loop(act, group, NG)

                @block.vector
                def _(dve):
                    st = Steps(dve, s_dv)
                    dve.sem_inc(s_done, 2)
                    dve.sem_inc(s_fbf, 2)
                    cw, cb = cwb[layer], cbb[layer]
                    tt = nc.vector.tensor_tensor

                    def group(i, par, use):
                        dve.wait_ge(s_fb, 5 * (i + 1))
                        dve.wait_ge(s_m[par], 16 * JG * (use + 1))
                        dve.wait_ge(s_halo, i + 2)
                        dve.sem_inc(s_tk, 1)
                        st.mark(nc.vector.copy_predicated(
                            S1[par][:], ms1[:, par].unsqueeze(2).to_broadcast([P, JG + 2, D]), M[par][:, 1:JG + 3, :]))
                        st.wait()
                        st.mark(tt(low[:], M[par][:, 0:JG + 2, :], S1[par][:], ALU.min))
                        st.mark(tt(high[:], M[par][:, 0:JG + 2, :], S1[par][:], ALU.max))
                        st.wait()
                        dve.sem_inc(s_done, 1)
                        mask = ms2[:, par].unsqueeze(2).to_broadcast([P, JG, D])
                        st.mark(nc.vector.copy_predicated(L2[par][:], mask, low[:, 2:JG + 2, :]))
                        st.mark(nc.vector.copy_predicated(H2[par][:], mask, high[:, 2:JG + 2, :]))
                        need(dve, s_sc[par], 16 * JG * use)
                        st.wait()
                        dve.sem_inc(s_tk, 1)
                        lo14, hi14 = low[:, 0:JG, :], high[:, 0:JG, :]
                        st.mark(tt(ob[par][:], lo14, L2[par][:], ALU.min))
                        st.mark(tt(A[:], lo14, L2[par][:], ALU.max))
                        st.wait()
                        st.mark(tt(L2[par][:], hi14, H2[par][:], ALU.min))
                        st.wait()
                        st.mark(tt(H2[par][:], hi14, H2[par][:], ALU.max))
                        st.mark(tt(lo14, A[:], L2[par][:], ALU.min))
                        st.wait()
                        st.mark(tt(A[:], A[:], L2[par][:], ALU.max))
                        st.mark(nc.vector.tensor_scalar(ob[par][:], ob[par][:], cw[:, 0:1], cb[:, 0:1],
                                                        ALU.mult, ALU.add))
                        for q, v in enumerate((lo14, A[:], H2[par][:])):
                            st.wait()
                            st.mark(nc.vector.scalar_tensor_tensor(ob[par][:], v, cw[:, q + 1:q + 2], ob[par][:],
                                                                   ALU.mult, ALU.add))
                        st.wait()
                        dve.sem_inc(s_o, 1)
                        dve.sem_inc(s_fbf, 1)

                    group_marks = 15

                    dve.wait_ge(s_m0, 48)
                    chunk_loop(dve, group, NG, st, group_marks)

        def statistics(layer, pool_work=None):
            n = f"st{layer}_"
            s_in = [sem(n + "in0"), sem(n + "in1")]
            s_fr = [sem(n + "fr0"), sem(n + "fr1")]
            s_u = sem(n + "u")
            s_q = sem(n + "q")
            s_pe = sem(n + "pe")
            s_dv = sem(n + "dve")
            s_rt = sem(n + "rt")
            c = ExitStack()
            with c:
                hb = [sb(f"{n}h{i}", [P, RT * D], F32, c) for i in range(2)]
                ob = [sb(f"{n}o{i}", [P, RT * D], F32, c) for i in range(2)]
                sq = [sb(f"{n}q{i}", [P, RT * D], F32, c) for i in range(2)]
                tot = sb(n + "tot", [P, 2, D], F32, c)
                var = sb(n + "var", [P, D], F32, c)
                rt = sb(n + "rt", [P, D], F32, c)
                psU = pb(n + "psU", [P, 512], F32, c)
                psQ = pb(n + "psQ", [P, 512], F32, c)
                block = c.enter_context(nc.Block())
                hv = h_tab[layer].rearrange("(c p t) f -> c p (t f)", p=P, t=RT)
                ov = o_tab[layer].rearrange("(c p t) f -> c p (t f)", p=P, t=RT)

                @block.sync
                def _(sp):
                    def load(i, par, use):
                        sp.wait_ge(s_fr[par], use + 1)
                        for t, v in ((hb, hv), (ob, ov)):
                            sp.dma_start(t[par][:], v[bass.ds(i, 1)].rearrange("c p n -> (c p) n")
                                         ).then_inc(s_in[par], 16)

                    chunk_loop(sp, load)

                if pool_work:
                    @block.gpsimd
                    def _(pool):
                        pool_work(pool, c)

                @block.vector
                def _(dve):
                    st = Steps(dve, s_dv)

                    def chunk(i, par, use):
                        dve.wait_ge(s_in[par], 32 * (use + 1))
                        nc.vector.scalar_tensor_tensor(ob[par][:], hb[par][:], ab[layer][:, 0:1], ob[par][:],
                                                       ALU.mult, ALU.add).then_inc(s_u, 1)

                    chunk_loop(dve, chunk)
                    dve.wait_ge(s_pe, NCH)
                    for q, ps in enumerate((psU, psQ)):
                        st.mark(nc.vector.tensor_reduce(tot[:, q, :], ps[:].rearrange("p (t f) -> p f t", f=D),
                                                        AX.X, ALU.add))
                    st.wait()
                    st.mark(nc.vector.tensor_scalar(tot[:], tot[:], 1.0 / N, None, ALU.mult))
                    st.wait()
                    st.mark(nc.vector.tensor_tensor(var[:], tot[:, 0, :], tot[:, 0, :], ALU.mult))
                    st.wait()
                    st.mark(nc.vector.tensor_tensor(var[:], tot[:, 1, :], var[:], ALU.subtract))
                    st.wait()
                    st.mark(nc.vector.tensor_scalar(var[:], var[:], 0.0, None, ALU.max))
                    st.wait()
                    dve.wait_ge(s_rt, 1)
                    st.mark(nc.vector.reciprocal(rt[:], rt[:]))
                    st.wait()
                    st.mark(nc.vector.tensor_tensor(bn_s[layer][:], rt[:], gb[layer][:], ALU.mult))
                    st.wait()
                    st.mark(nc.vector.tensor_tensor(var[:], tot[:, 0, :], bn_s[layer][:], ALU.mult))
                    st.wait()
                    st.mark(nc.vector.tensor_tensor(bn_t[layer][:], beb[layer][:], var[:], ALU.subtract))
                    st.wait()

                @block.scalar
                def _(act):
                    def chunk(i, par, use):
                        act.wait_ge(s_u, i + 1)
                        act.wait_ge(s_fr[par], use + 1)
                        nc.scalar.activation(sq[par][:], ob[par][:], ACT.Square).then_inc(s_q, 1)

                    chunk_loop(act, chunk)
                    act.wait_ge(s_dv, 6)
                    nc.scalar.activation(rt[:], var[:], ACT.Sqrt, bias=epsc[:, 0:1]).then_inc(s_rt, 1)

                @block.tensor
                def _(pe):
                    for par in range(2):
                        pe.sem_inc(s_fr[par], 1)

                    def chunk(i, par, use):
                        first, last = (isinstance(i, int) and i == v for v in (0, NCH - 1))
                        w = ones_last if last else ones
                        for t, s, ps in ((ob, s_u, psU), (sq, s_q, psQ)):
                            pe.wait_ge(s, i + 1)
                            for q in range(2):
                                ins = nc.tensor.matmul(ps[:], w[:], t[par][:, 512 * q:512 * (q + 1)],
                                                       start=first and q == 0, stop=last and q == 1,
                                                       skip_group_check=True)
                        ins.then_inc(s_pe, 1)
                        pe.wait_ge(s_pe, i + 1)
                        pe.sem_inc(s_fr[par], 1)

                    chunk_loop(pe, chunk)

        bn_s = [sb(f"bn_s{i}", [P, D]) for i in range(2)]
        bn_t = [sb(f"bn_t{i}", [P, D]) for i in range(2)]

        def apply0(pool_work):
            s_in = [sem("ap_in0"), sem("ap_in1")]
            s_out = [sem("ap_out0"), sem("ap_out1")]
            s_dv = sem("ap_dve")
            s_r = sem("ap_rows")
            c = ExitStack()
            with c:
                hb = [sb(f"ap_h{i}", [P, RT, D], F32, c) for i in range(2)]
                ob = [sb(f"ap_o{i}", [P, RT, D], F32, c) for i in range(2)]
                block = c.enter_context(nc.Block())
                hv, ov, wv = (t.rearrange("(c p t) f -> c p t f", p=P, t=RT) for t in (h_tab[0], o_tab[0], h_tab[1]))

                @block.sync
                def _(sp):
                    def load(i, par, use):
                        need(sp, s_out[par], 16 * use)
                        for t, v in ((hb, hv), (ob, ov)):
                            sp.dma_start(t[par][:], v[bass.ds(i, 1)].rearrange("c p t f -> (c p) t f")
                                         ).then_inc(s_in[par], 16)

                    chunk_loop(sp, load)

                @block.gpsimd
                def _(pool):
                    pool_work(pool, c)

                @block.scalar
                def _(act):
                    def store(i, par, use):
                        act.wait_ge(s_r, i + 1)
                        act.dma_start(wv[bass.ds(i, 1)].rearrange("c p t f -> (c p) t f"), ob[par][:]
                                      ).then_inc(s_out[par], 16)

                    chunk_loop(act, store)
                    act.wait_ge(s_out[0], 16 * (NCH // 2 + 1))
                    act.wait_ge(s_out[1], 16 * (NCH // 2))

                @block.vector
                def _(dve):
                    st = Steps(dve, s_dv)
                    sc = bn_s[0][:].unsqueeze(1).to_broadcast([P, RT, D])
                    sh = bn_t[0][:].unsqueeze(1).to_broadcast([P, RT, D])

                    def chunk(i, par, use):
                        dve.wait_ge(s_in[par], 32 * (use + 1))
                        normalise(nc, st, hb[par], ob[par][:], ab[0], sc, sh)
                        st.wait()
                        dve.sem_inc(s_r, 1)

                    chunk_loop(dve, chunk, NCH, st, 4)

        def apply1():
            s_in = [sem("a1_in0"), sem("a1_in1")]
            s_out = [sem("a1_out0"), sem("a1_out1")]
            s_free = sem("a1_free")
            s_dv = sem("a1_dve")
            s_r = sem("a1_rows")
            s_cp = sem("a1_cp")
            s_tk = sem("a1_tk")
            s_pad = sem("a1_pad")
            c = ExitStack()
            with c:
                xb = [sb(f"a1_x{i}", [P, RT, D], F32, c) for i in range(2)]
                hb = [sb(f"a1_h{i}", [P, RT, D], F32, c) for i in range(2)]
                ob = [sb(f"a1_o{i}", [P, RT, D], F32, c) for i in range(2)]
                rb = [sb(f"a1_r{i}", [P, RT, IDW], F32, c) for i in range(2)]
                number = sb("a1_number", [P, RT], F32, c)
                pi = sb("a1_pi", [P, 2, RT], I32, c)
                block = c.enter_context(nc.Block())
                hv, ov = (t.rearrange("(c t p) f -> c p t f", p=P, t=RT) for t in (h_tab[1], o_tab[1]))
                m = (NCH - 1) * P * RT
                xv = x[0:m, :].rearrange("(c t p) f -> c p t f", p=P, t=RT)
                full = (N - m) // P
                part = N - m - full * P

                @block.sync
                def _(sp):
                    def load(i, par, use):
                        last = isinstance(i, int) and i == NCH - 1
                        sp.wait_ge(s_free, i + 1)
                        for t, v in ((hb, hv), (ob, ov)) + (() if last else ((xb, xv),)):
                            sp.dma_start(t[par][:], v[bass.ds(i, 1)].rearrange("c p t f -> (c p) t f")
                                         ).then_inc(s_in[par], 16)
                        if last:
                            sp.wait_ge(s_pad, 1)
                            sp.dma_start(xb[par][:, 0:full, :], x[m:m + full * P, :].rearrange("(t p) f -> p t f", p=P)
                                         ).then_inc(s_in[par], 16)
                            sp.dma_start(xb[par][0:part, full, :], x[m + full * P:N, :]).then_inc(s_in[par], 16)

                    chunk_loop(sp, load)

                @block.vector
                def _(dve):
                    st = Steps(dve, s_dv)
                    sc = bn_s[1][:].unsqueeze(1).to_broadcast([P, RT, D])
                    sh = bn_t[1][:].unsqueeze(1).to_broadcast([P, RT, D])
                    st.mark(nc.vector.tensor_scalar(number[:], iota_w[:, 0:RT], float(P), iota_p[:, 0:1],
                                                    ALU.mult, ALU.add))
                    for par in range(2):
                        st.mark(nc.vector.memset(rb[par][:, :, D:IDW], 0.0))
                    st.wait()
                    dve.sem_inc(s_free, 2)

                    def chunk(i, par, use):
                        last = isinstance(i, int) and i == NCH - 1
                        dve.wait_ge(s_in[par], 48 * (use + 1) + (16 if last else 0))
                        normalise(nc, st, hb[par], ob[par][:], ab[1], sc, sh)
                        need(dve, s_out[par], 16 * RT * use)
                        st.mark(nc.vector.tensor_copy(rb[par][:, :, D].bitcast(I32), number[:]))
                        st.wait()
                        st.mark(nc.vector.tensor_scalar(number[:], number[:], float(P * RT), None, ALU.add))
                        st.wait()
                        st.mark(nc.vector.tensor_tensor(rb[par][:, :, 0:D], ob[par][:], xb[par][:], ALU.add))
                        st.wait()
                        dve.sem_inc(s_r, 1)
                        dve.sem_inc(s_free, 1)

                    chunk_loop(dve, chunk, NCH, st, 7)

                @block.gpsimd
                def _(pool):
                    st = Steps(pool, s_cp)
                    def chunk(i, par, use):
                        if isinstance(i, int) and i == NCH - 1:
                            pool.wait_ge(s_free, NCH - 2 + 1)
                            nc.gpsimd.memset(xb[0][:], 0.0).then_inc(s_pad, 1)
                        need(pool, s_out[par], 16 * RT * use)
                        st.mark(nc.gpsimd.tensor_copy(pi[:, par], node_pos[:, bass.ds(RT * i, RT)]))
                        st.wait()
                        pool.wait_ge(s_r, i + 1)
                        pool.sem_inc(s_tk, 1)
                        for t in range(RT):
                            pool.indirect_dma_start(x2_tab, bass.IndirectOffsetOnAxis(ap=pi[:, par, t:t + 1], axis=0),
                                                    rb[par][:, t, :], None).then_inc(s_out[par], 16)

                    chunk_loop(pool, chunk, NCH, st, 1)
                    pool.wait_ge(s_out[0], 16 * RT * (NCH // 2 + 1))
                    pool.wait_ge(s_out[1], 16 * RT * (NCH // 2))

        convolve(0)
        statistics(0, lambda pool, c: pool_columns(pool, "lks", c, node_tab, src_at, look, False))
        apply0(lambda pool, c: pool_columns(pool, "lkd", c, node_tab, dst_at, pair, False))
        s_dv4 = sem("s4_dve")
        c4 = ExitStack()
        with c4:
            pf = sb("pf", [P, EC], F32, c4)
            pi4 = sb("pi4", [P, EC], I32, c4)
            pj4 = sb("pj4", [P, EC], I32, c4)
            pg = sb("pg", [P, EC], F32, c4)
            ph = sb("ph", [P, EC], F32, c4)
            block = c4.enter_context(nc.Block())

            @block.vector
            def _(dve):
                st = Steps(dve, s_dv4)

                def do(ins):
                    st.mark(ins)
                    st.wait()

                do(nc.vector.tensor_copy(pf[:], look[:, :, 0]))
                do(nc.vector.tensor_tensor(pf[:], pf[:], occ[:], ALU.add))
                do(nc.vector.tensor_copy(pi4[:], pf[:]))
                do(nc.vector.tensor_scalar(pj4[:], pi4[:], P - 1, None, ALU.bitwise_and))
                do(nc.vector.tensor_copy(pg[:], pj4[:]))
                do(nc.vector.tensor_scalar(pj4[:], pi4[:], 7, None, ALU.logical_shift_right))
                do(nc.vector.tensor_copy(ph[:], pj4[:]))
                do(nc.vector.scalar_tensor_tensor(pf[:], pg[:], float(EC), ph[:], ALU.mult, ALU.add))
                do(nc.vector.tensor_copy(pg[:], edge_src[:, 0:EC]))
                do(nc.vector.tensor_scalar(pg[:], pg[:], float(NPAD), None, ALU.is_ge))
                do(nc.vector.scalar_tensor_tensor(sort_at[:], pg[:], float(FAR), pf[:], ALU.mult, ALU.add))
                do(nc.vector.tensor_copy(pair[:, :, 0], pair[:, :, 1]))
                do(nc.vector.tensor_copy(pair[:, :, 1], look[:, :, 1]))
        convolve(1)
        statistics(1, lambda pool, c: pool_columns(pool, "srt", c, sort_tab, sort_at, pair, True))
        apply1()
        W_msg, b_msg, W_ih, W_hh, b_ih, b_hh = gru

        wih = sb("wih", [P, 3 * D])
        whh = sb("whh", [P, 3 * D])
        wmsg = sb("wmsg", [P, D])
        bmsg = sb("bmsg", [P, D])
        bih = sb("bih", [P, 3])
        bhh = sb("bhh", [P, 3])
        brz = sb("brz", [P, 2])
        agg = sb("agg", [P, EPAD + CW])
        sorted_ = sb("sorted", [P, EC, 2], I32)
        base = sb("base", [1, EC], I32)
        lrank = sb("lrank", [P, EC])
        srow = sb("srow", [P, EC], I32)
        s_hst = [sem("g_hst0"), sem("g_hst1")]
        s_mst = [sem("g_mst0"), sem("g_mst1")]
        NPC = NPAD // CW
        NB = NPC // 2
        FIRST = [NB - NB // 2, NB // 2]
        TPC = CW // P
        x2v = x2_tab.rearrange("(c p t) w -> c p t w", p=P, t=TPC)
        htv = ht_tab.rearrange("f (c n) -> f c n", n=CW)
        msgv = [t.rearrange("(c p t) f -> c p (t f)", p=P, t=TPC) for t in msg_tab]

        s_w = sem("i_w")
        s_xin = [sem("i_x0"), sem("i_x1")]
        s_stat = sem("i_stat")
        s_root = sem("i_root")
        s_cols = sem("i_cols")
        s_relu = sem("i_relu")
        s_tr = sem("i_tr")
        s_hT = sem("i_hT")
        s_pm = sem("i_pm")
        s_me = sem("i_me")
        s_dv = sem("i_dve")
        s_srt = sem("i_sorted")
        s_pl = sem("i_pool")
        s_tk = sem("i_tick")
        c5 = ExitStack()
        with c5:
            xb = [sb(f"i_x{i}", [P, 2, TPC, IDW], F32, c5) for i in range(2)]
            rb = [sb(f"i_r{i}", [P, 2, TPC, D], F32, c5) for i in range(2)]
            hT = [sb(f"i_hT{i}", [P, 2, CW], F32, c5) for i in range(2)]
            mb = [sb(f"i_m{i}", [P, 2, TPC, D], F32, c5) for i in range(2)]
            stats = sb("i_stats", [P, 2 * TPC, 6], F32, c5)
            mv = sb("i_mv", [P, 2, 2 * TPC, 2], F32, c5)
            root = sb("i_root", [P, 2, 2 * TPC], F32, c5)
            cols = sb("i_cols", [P, 2, 2, 2 * TPC], F32, c5)
            rankf = sb("i_rank", [P, EC], F32, c5)
            psT = [pb(f"i_psT{i}", [P, TPC, P], F32, c5) for i in range(2)]
            psM = [pb(f"i_psM{i}", [P, TPC, D], F32, c5) for i in range(2)]
            psR = pb("i_psR", [P, EC], F32, c5)
            block = c5.enter_context(nc.Block())

            @block.sync
            def _(sp):
                loads = [sp.dma_start(sorted_[:], sort_tab.rearrange("(p j) w -> p j w", j=EC)),
                         sp.dma_start(wih[:], W_ih), sp.dma_start(whh[:], W_hh), sp.dma_start(wmsg[:], W_msg),
                         sp.dma_start(bmsg[:], b_msg.partition_broadcast(P))]
                for t, v in ((bih, b_ih), (bhh, b_hh)):
                    loads.append(sp.dma_start(t[:], v.rearrange("(g p) -> p g", p=P), allow_slow_non_contiguous=True))
                for ins in loads:
                    ins.then_inc(s_w, 16)

                def chunk(i, par, use):
                    need(sp, s_relu, 2 * TPC * (i - 1))
                    sp.dma_start(xb[par][:], x2v[bass.ds(2 * i, 2)].rearrange("c p t w -> p c t w")
                                 ).then_inc(s_xin[par], 16)
                    if not isinstance(i, int) or i >= 2:
                        store_h(i - 2, par)
                    if not isinstance(i, int) or i >= 3:
                        store_m(i - 3, 1 - par)

                def store_h(i, par):
                    sp.wait_ge(s_hT, 2 * (i + 1))
                    sp.dma_start(htv[:, bass.ds(2 * i, 2), :], hT[par][:]).then_inc(s_hst[par], 16)

                def store_m(i, par):
                    sp.wait_ge(s_me, 2 * (i + 1))
                    sp.dma_start(msgv[0][bass.ds(2 * i, 2)].rearrange("c p n -> p c n"),
                                 mb[par][:].rearrange("p c t f -> p c (t f)")).then_inc(s_mst[par], 16)

                chunk_loop(sp, chunk, NB, peel=4)
                store_h(NB - 2, 1)
                store_m(NB - 3, 0)
                store_h(NB - 1, 0)
                store_m(NB - 2, 1)
                store_m(NB - 1, 0)
                for par in range(2):
                    sp.wait_ge(s_hst[par], 16 * FIRST[par])
                    sp.wait_ge(s_mst[par], 16 * FIRST[par])

            @block.gpsimd
            def _(pool):
                nc.gpsimd.memset(agg[:], 0.0).then_inc(s_pl, 1)

            @block.vector
            def _(dve):
                st = Steps(dve, s_dv)

                def do(ins):
                    st.mark(ins)
                    st.wait()

                dve.wait_ge(s_w, 16 * 7)
                do(nc.vector.tensor_tensor(brz[:], bih[:, 0:2], bhh[:, 0:2], ALU.add))
                do(nc.vector.tensor_copy(srow[:], sorted_[:, :, 0]))
                do(nc.vector.tensor_copy(rankf[:], sorted_[:, :, 1]))
                do(nc.vector.tensor_scalar(rankf[:], rankf[:], float(-EPAD), None, ALU.add))
                do(nc.vector.tensor_copy(base[:], rankf[0:1, :]))
                dve.sem_inc(s_srt, 1)
                dve.wait_ge(s_srt, 2)
                do(nc.vector.tensor_tensor(lrank[:], psR[:], rankf[:], ALU.subtract))

                def evacuate(i, par, use, h):
                    dve.wait_ge(s_pm, 2 * i + h + 1)
                    need(dve, s_mst[par], 16 * use)
                    nc.vector.tensor_tensor(mb[par][:, h], psM[h][:], bmsg[:].unsqueeze(1).to_broadcast([P, TPC, D]),
                                            ALU.add).then_inc(s_me, 1)

                def chunk(i, par, use):
                    dve.wait_ge(s_xin[par], 16 * (use + 1))
                    for t in range(2 * TPC):
                        st.mark(nc.vector.bn_stats(stats[:, t, :], xb[par][:, t // TPC, t % TPC, 0:D]))
                    st.wait()
                    dve.sem_inc(s_tk, 1)
                    for t in range(2 * TPC):
                        st.mark(nc.vector.bn_aggr(mv[:, par, t, :], stats[:, t, :]))
                    st.wait()
                    dve.sem_inc(s_stat, 1)
                    dve.wait_ge(s_root, i + 1)
                    st.mark(nc.vector.reciprocal(cols[:, par, 0, :], root[:, par, :]))
                    st.wait()
                    st.mark(nc.vector.scalar_tensor_tensor(cols[:, par, 1, :], mv[:, par, :, 0], -1.0,
                                                           cols[:, par, 0, :], ALU.mult, ALU.mult))
                    st.wait()
                    dve.sem_inc(s_cols, 1)
                    if not isinstance(i, int) or i >= 2:
                        for h in range(2):
                            evacuate(i - 2, *behind(par, use, 2), h)

                chunk_loop(dve, chunk, NB, st, 4 * TPC + 2)
                for i in (NB - 2, NB - 1):
                    for h in range(2):
                        evacuate(i, i % 2, i // 2, h)

            @block.scalar
            def _(act):
                def copy_state(i, par, use, h):
                    act.wait_ge(s_tr, TPC * (2 * i + h + 1))
                    need(act, s_hst[par], 16 * use)
                    need(act, s_pm, 2 * i + h - 3)
                    nc.scalar.activation(hT[par][:, h].rearrange("f (p t) -> f t p", t=TPC), psT[h][:], ACT.Copy
                                         ).then_inc(s_hT, 1)

                def chunk(i, par, use):
                    act.wait_ge(s_stat, i + 1)
                    nc.scalar.activation(root[:, par], mv[:, par, :, 1], ACT.Sqrt, bias=epsc[:, 0:1]
                                         ).then_inc(s_root, 1)
                    if not isinstance(i, int) or i >= 1:
                        for h in range(2):
                            copy_state(i - 1, *behind(par, use, 1), h)
                    act.wait_ge(s_cols, i + 1)
                    need(act, s_tr, 2 * TPC * (i - 1))
                    for t in range(2 * TPC):
                        nc.scalar.activation(rb[par][:, t // TPC, t % TPC, :], xb[par][:, t // TPC, t % TPC, 0:D],
                                             ACT.Relu, bias=cols[:, par, 1, t:t + 1], scale=cols[:, par, 0, t:t + 1]
                                             ).then_inc(s_relu, 1)

                chunk_loop(act, chunk, NB, peel=4)
                for h in range(2):
                    copy_state(NB - 1, 0, NB // 2, h)

            @block.tensor
            def _(pe):
                pe.wait_ge(s_srt, 1)
                nc.tensor.matmul(psR[:], row0[:], rankf[:], start=True, stop=True).then_inc(s_srt, 1)
                pe.wait_ge(s_w, 16 * 7)

                def messages(i, par, h):
                    pe.wait_ge(s_hT, 2 * i + h + 1)
                    need(pe, s_me, 2 * i + h - 1)
                    for t in range(TPC):
                        ins = nc.tensor.matmul(psM[h][:, t, :], hT[par][:, h, t:CW:TPC], wmsg[:], start=True, stop=True)
                    ins.then_inc(s_pm, 1)

                def chunk(i, par, use):
                    for h in range(2):
                        pe.wait_ge(s_relu, TPC * (2 * i + h + 1))
                        need(pe, s_hT, 2 * i + h - 1)
                        for t in range(TPC):
                            nc.tensor.transpose(psT[h][:, t, :], rb[par][:, h, t, :], ident[:]).then_inc(s_tr, 1)
                    if not isinstance(i, int) or i >= 1:
                        for h in range(2):
                            messages(i - 1, 1 - par, h)

                chunk_loop(pe, chunk, NB)
                for h in range(2):
                    messages(NB - 1, 0, h)

        HALF = NPC // 2
        TQ = EC // HALF
        s_hin = [sem("r_hin0"), sem("r_hin1")]
        s_g = [sem("r_g0"), sem("r_g1")]
        s_ib = sem("r_ib")
        s_clr = sem("r_clear")
        s_hn, s_pr, s_pz, s_pi = sem("r_hn"), sem("r_pr"), sem("r_pz"), sem("r_pi")
        s_r, s_z, s_n = sem("r_r"), sem("r_z"), sem("r_n")
        s_t1, s_t2 = sem("r_t1"), sem("r_t2")
        s_d1, s_d2, s_h = sem("r_d1"), sem("r_d2"), sem("r_h")
        s_di = sem("r_dist")
        s_sb, s_sel, s_ev = sem("r_sb"), sem("r_sel"), sem("r_ev")
        s_pm, s_me = sem("r_pm"), sem("r_me")
        s_x2 = [sem("r_x0"), sem("r_x1")]
        s_fin = [sem("r_fin0"), sem("r_fin1")]
        s_tk = sem("r_tick")
        c6 = ExitStack()
        with c6:
            hin = [sb(f"r_hin{i}", [P, CW], F32, c6) for i in range(2)]
            hnew = [sb(f"r_hnew{i}", [P, CW], F32, c6) for i in range(2)]
            rs = [sb(f"r_r{i}", [P, CW], F32, c6) for i in range(2)]
            zs = [sb(f"r_z{i}", [P, CW], F32, c6) for i in range(2)]
            ns = [sb(f"r_n{i}", [P, CW], F32, c6) for i in range(2)]
            ts = [sb(f"r_t{i}", [P, CW], F32, c6) for i in range(2)]
            dsb = sb("r_d", [P, CW], F32, c6)
            mb = [sb(f"r_m{i}", [P, TPC, D], F32, c6) for i in range(2)]
            G = [sb(f"r_G{i}", [P, TQ, D], F32, c6) for i in range(2)]
            ib = sb("r_ib", [P, 2, TQ], I32, c6)
            dist = sb("r_dist", [P, TQ, SW], F32, c6)
            sel = sb("r_sel", [P, TQ, SW], F32, c6)
            zero = sb("r_zero", [P, CW], F32, c6)
            x2b = [sb(f"r_x2{i}", [P, TPC, IDW], F32, c6) for i in range(2)]
            psHN = [pb(f"r_psHN{i}", [P, CW], F32, c6) for i in range(2)]
            psR = pb("r_psR", [P, CW], F32, c6)
            psZ = pb("r_psZ", [P, CW], F32, c6)
            psI = pb("r_psI", [P, CW], F32, c6)
            psM = pb("r_psM", [P, TPC, D], F32, c6)
            psS = [pb(f"r_psS{i}", [P, 2, 256], F32, c6) for i in range(2)]
            block = c6.enter_context(nc.Block())

            def steps(eng, step):
                def two(k):
                    step(2 * k, 0, 1, False)
                    step(2 * k + 1, 1, 0, False)

                engine_loop(eng, STEPS // 2, two)
                step(STEPS - 1, 0, 1, True)

            @block.sync
            def _(sp):
                def step(s, src_m, dst_m, last):
                    done = NPC * s

                    def load(c, par):
                        sp.dma_start(hin[par][:], htv[:, bass.ds(c, 1), :].rearrange("f c n -> f (c n)")
                                     ).then_inc(s_hin[par], 16)

                    def store_m(c, par):
                        sp.wait_ge(s_me, done + c + 2)
                        sp.dma_start(msgv[dst_m][bass.ds(c, 1)].rearrange("c p n -> (c p) n"),
                                     mb[par][:].rearrange("p t f -> p (t f)")).then_inc(s_mst[par], 16)

                    def load_x2(c, par, use):
                        need(sp, s_fin[par], 16 * TPC * use)
                        sp.dma_start(x2b[par][:], x2v[bass.ds(c, 1)].rearrange("c p t w -> (c p) t w")
                                     ).then_inc(s_x2[par], 16)

                    def chunk(c, par, use):
                        sp.wait_ge(s_d1, done + c + 1)
                        sp.sem_inc(s_tk, 1)
                        if not isinstance(c, int) or c < NPC - 2:
                            load(c + 2, par)
                        if not last:
                            sp.wait_ge(s_h, done + c + 3)
                            sp.dma_start(htv[:, bass.ds(c, 1), :].rearrange("f c n -> f (c n)"), hnew[par][:]
                                         ).then_inc(s_hst[par], 16)
                        if not isinstance(c, int) or c >= 1:
                            if not last:
                                store_m(c - 1, 1 - par)
                            elif not isinstance(c, int) or c < NPC - 1:
                                load_x2(c + 1, *behind(par, use, -1))

                    load(0, 0)
                    load(1, 1)
                    if last:
                        load_x2(0, 0, 0)
                        load_x2(1, 1, 0)
                    two_halves(sp, chunk, chunk, tail=2)
                    if not last:
                        store_m(NPC - 1, 1)

                steps(sp, step)
                for par in range(2):
                    sp.wait_ge(s_hst[par], 16 * (FIRST[par] + HALF * (STEPS - 1)))
                    sp.wait_ge(s_mst[par], 16 * (FIRST[par] + HALF * (STEPS - 1)))

            @block.gpsimd
            def _(pool):
                ids = [[x2b[par][:, t, D:D + 1].bitcast(I32) for t in range(TPC)] for par in range(2)]
                nc.gpsimd.memset(zero[:], 0.0).then_inc(s_clr, 1)
                pool.wait_ge(s_clr, 1)

                def step(s, src_m, dst_m, last):
                    for par in range(2):
                        pool.wait_ge(s_mst[par], 16 * (FIRST[par] + HALF * s))

                    def scatter(c, par):
                        pool.wait_ge(s_me, NPC * s + c + 2)
                        pool.sem_inc(s_tk, 1)
                        for t in range(TPC):
                            pool.indirect_dma_start(out, bass.IndirectOffsetOnAxis(ap=ids[par][t], axis=0),
                                                    mb[par][:, t, :], None, bounds_check=N - 1, oob_is_err=False
                                                    ).then_inc(s_fin[par], 16)

                    def gather(c, par):
                        pool.wait_ge(s_sel, TQ * (HALF * s + c + 1))
                        pool.sem_inc(s_tk, 1)
                        nc.gpsimd.tensor_copy(ib[:, par], srow[:, bass.ds(TQ * c, TQ)]).then_inc(s_ib, 1)
                        pool.wait_ge(s_ib, HALF * s + c + 1)
                        pool.sem_inc(s_tk, 1)
                        for q in range(TQ):
                            pool.indirect_dma_start(G[par][:, q, :], None, msg_tab[src_m],
                                                    bass.IndirectOffsetOnAxis(ap=ib[:, par, q:q + 1], axis=0)
                                                    ).then_inc(s_g[par], 16)

                    def clear(c):
                        pool.wait_ge(s_pi, HALF * s + c - HALF + 1)
                        pool.sem_inc(s_tk, 1)
                        nc.gpsimd.tensor_copy(agg[:, bass.ds(CW * (c - HALF), CW)], zero[:]).then_inc(s_clr, 1)

                    def first(c, par, use):
                        gather(c, par)
                        if last and not (isinstance(c, int) and c < 2):
                            scatter(c - 2, par)

                    def second(c, par, use):
                        if last:
                            scatter(c - 2, par)
                        else:
                            clear(c)

                    two_halves(pool, first, second)
                    if last:
                        scatter(NPC - 2, 0)
                        scatter(NPC - 1, 1)

                steps(pool, step)
                for par in range(2):
                    pool.wait_ge(s_fin[par], 16 * TPC * HALF)

            @block.tensor
            def _(pe):
                def step(s, src_m, dst_m, last):
                    done = NPC * s

                    def finish(c, par):
                        pe.wait_ge(s_h, done + c + 3)
                        pe.wait_ge(s_me, done + c + 1)
                        for t in range(TPC):
                            if last:
                                ins = nc.tensor.transpose(psM[:, t, :], hnew[par][:, t:CW:TPC], ident[:])
                            else:
                                ins = nc.tensor.matmul(psM[:, t, :], hnew[par][:, t:CW:TPC], wmsg[:],
                                                       start=True, stop=True)
                        ins.then_inc(s_pm, 1)

                    def gates(c, par, use, edges):
                        pe.wait_ge(s_hin[par], 16 * (HALF * s + use + 1))
                        pe.wait_ge(s_t1, done + c + 1)
                        nc.tensor.matmul(psHN[par][:], whh[:, 2 * D:3 * D], hin[par][:], start=True, stop=True
                                         ).then_inc(s_hn, 1)
                        for g, ps, free, sig in ((0, psR, s_r, s_pr), (1, psZ, s_z, s_pz)):
                            pe.wait_ge(free, done + c + 1)
                            ins = nc.tensor.matmul(ps[:], whh[:, g * D:(g + 1) * D], hin[par][:], start=True,
                                                   stop=not edges)
                            if edges:
                                ins = nc.tensor.matmul(ps[:], wih[:, g * D:(g + 1) * D],
                                                       agg[:, bass.ds(CW * (c - HALF), CW)], start=False, stop=True)
                            ins.then_inc(sig, 1)
                        if edges:
                            pe.wait_ge(s_t2, HALF * s + c - HALF + 1)
                            nc.tensor.matmul(psI[:], wih[:, 2 * D:3 * D], agg[:, bass.ds(CW * (c - HALF), CW)],
                                             start=True, stop=True).then_inc(s_pi, 1)

                    def tiles(c, par, use):
                        pe.wait_ge(s_g[par], 16 * TQ * ((25 - par) * s + use + 1))
                        pe.wait_ge(s_sb, HALF * s + c + 1)
                        pe.wait_ge(s_ev, TQ * (HALF * s + c + 1))
                        for q in range(TQ):
                            nc.tensor.matmul(psS[q // 2][:, q % 2, 0:SW], G[par][:, q, :], sel[:, q, :],
                                             start=True, stop=True).then_inc(s_sel, 1)

                    def first(c, par, use):
                        gates(c, par, use, False)
                        if not (isinstance(c, int) and c == 0):
                            finish(c - 1, 1 - par)
                        tiles(c, par, use)

                    def second(c, par, use):
                        if isinstance(c, int) and c == HALF:
                            pe.wait_ge(s_ev, EC * (s + 1) + TQ)
                        gates(c, par, use, True)
                        finish(c - 1, 1 - par)

                    two_halves(pe, first, second)
                    finish(NPC - 1, 1)

                steps(pe, step)

            @block.scalar
            def _(act):
                act.sem_inc(s_r, 1)
                act.sem_inc(s_z, 1)

                def step(s, src_m, dst_m, last):
                    done = NPC * s

                    def select(c):
                        act.wait_ge(s_sb, HALF * s + c)
                        for q in range(TQ):
                            nc.scalar.activation(dist[:, q, :], iota_w[:, 0:SW], ACT.Abs,
                                                 bias=lrank[:, bass.ds(TQ * c + q, 1)]).then_inc(s_di, 1)
                        act.wait_ge(s_di, TQ * (HALF * s + c + 1))
                        act.wait_ge(s_sel, TQ * (HALF * s + c + 2))
                        nc.scalar.activation(sel[:], dist[:], ACT.Relu, bias=1.0, scale=-1.0).then_inc(s_sb, 1)

                    def chunk(c, par, edges):
                        if not edges:
                            select(c)
                        act.wait_ge(s_pr, done + c + 1)
                        nc.scalar.activation(rs[par][:], psR[:], ACT.Sigmoid, bias=brz[:, 0:1]).then_inc(s_r, 1)
                        act.wait_ge(s_pz, done + c + 1)
                        act.wait_ge(s_d2, done + c)
                        nc.scalar.activation(zs[par][:], psZ[:], ACT.Sigmoid, bias=brz[:, 1:2]).then_inc(s_z, 1)
                        act.wait_ge(s_h, done + c + 1)
                        if edges:
                            act.wait_ge(s_t2, HALF * s + c - HALF + 2)
                        else:
                            act.wait_ge(s_t1, done + c + 3)
                        nc.scalar.activation(ns[par][:], ts[par][:], ACT.Tanh, bias=bih[:, 2:3]).then_inc(s_n, 1)

                    two_halves(act, lambda c, par, use: chunk(c, par, False), lambda c, par, use: chunk(c, par, True))

                steps(act, step)

            @block.vector
            def _(dve):
                dve.sem_inc(s_t1, 2)
                dve.sem_inc(s_t2, 1)
                dve.sem_inc(s_d2, 1)
                dve.sem_inc(s_me, 1)
                dve.sem_inc(s_h, 2)
                dve.sem_inc(s_sel, 2 * TQ)
                dve.sem_inc(s_ev, TQ)
                dve.wait_ge(s_clr, 1)

                def step(s, src_m, dst_m, last):
                    done = NPC * s
                    chunks = HALF * s

                    def ranks(c):
                        _, at = nc.values_load_multi_w_load_instructions(
                            base[0:1, bass.ds(TQ * c, TQ)], [mybir.EngineType.DVE], min_val=0, max_val=E,
                            skip_runtime_bounds_check_because="ranks of sources, counted in stage 3, are within 0 .. E")
                        return at

                    def add(c, q, at):
                        if q == 0:
                            dve.wait_ge(s_sel, TQ * (chunks + c + 3))
                        dve.wait_ge(s_ev, TQ * (chunks + c + 1) + q)
                        nc.vector.tensor_tensor(agg[:, bass.ds(at[q], SW)], psS[q // 2][:, q % 2, 0:SW],
                                                agg[:, bass.ds(at[q], SW)], ALU.add).then_inc(s_ev, 1)

                    def evacuate(c, par, use):
                        dve.wait_ge(s_pm, done + c + 1)
                        if last:
                            dve.wait_ge(s_x2[par], 16 * (use + 1))
                            need(dve, s_fin[par], 16 * TPC * use)
                            other = x2b[par][:, :, 0:D]
                        else:
                            dve.wait_ge(s_mst[par], 16 * (FIRST[par] + HALF * s + use))
                            other = bmsg[:].unsqueeze(1).to_broadcast([P, TPC, D])
                        nc.vector.tensor_tensor(mb[par][:], psM[:], other, ALU.add).then_inc(s_me, 1)

                    def hidden(c, par, edges):
                        dve.wait_ge(s_hn, done + c + 1)
                        dve.wait_ge(s_r, done + c + 2)
                        nc.vector.scalar_tensor_tensor(ts[par][:], psHN[par][:], bhh[:, 2:3], rs[par][:],
                                                       ALU.add, ALU.mult).then_inc(s_t1, 1)
                        if edges:
                            dve.wait_ge(s_pi, chunks + c - HALF + 1)
                            dve.wait_ge(s_t1, done + c + 3)
                            nc.vector.tensor_tensor(ts[par][:], ts[par][:], psI[:], ALU.add).then_inc(s_t2, 1)

                    def update(c, par, use, between=()):
                        fill = list(between) + [None] * 2
                        dve.wait_ge(s_n, done + c + 1)
                        dve.wait_ge(s_d2, done + c + 1)
                        nc.vector.tensor_tensor(dsb[:], hin[par][:], ns[par][:], ALU.subtract).then_inc(s_d1, 1)
                        if fill[0]:
                            fill[0]()
                        dve.wait_ge(s_z, done + c + 2)
                        dve.wait_ge(s_d1, done + c + 1)
                        nc.vector.tensor_tensor(dsb[:], dsb[:], zs[par][:], ALU.mult).then_inc(s_d2, 1)
                        if fill[1]:
                            fill[1]()
                        dve.wait_ge(s_d2, done + c + 2)
                        if not last:
                            dve.wait_ge(s_hst[par], 16 * (FIRST[par] + HALF * s + use))
                        nc.vector.tensor_tensor(hnew[par][:], ns[par][:], dsb[:], ALU.add).then_inc(s_h, 1)

                    def first(c, par, use):
                        if isinstance(c, int) and c == 0:
                            hidden(c, par, False)
                            return
                        at = ranks(c - 1)
                        if isinstance(c, int) and c == 1:
                            dve.wait_ge(s_clr, chunks + 1)
                        update(c - 1, *behind(par, use, 1), (lambda: add(c - 1, 0, at), lambda: add(c - 1, 1, at)))
                        if not isinstance(c, int) or c >= 2:
                            evacuate(c - 2, *behind(par, use, 2))
                        hidden(c, par, False)
                        add(c - 1, 2, at)
                        add(c - 1, 3, at)

                    def second(c, par, use):
                        if isinstance(c, int) and c == HALF:
                            at = ranks(c - 1)
                            for q in range(TQ):
                                add(c - 1, q, at)
                        update(c - 1, *behind(par, use, 1), (lambda: evacuate(c - 2, *behind(par, use, 2)),))
                        hidden(c, par, True)

                    if last:
                        for par in range(2):
                            dve.wait_ge(s_mst[par], 16 * (FIRST[par] + HALF * (STEPS - 1)))
                            dve.wait_ge(s_hst[par], 16 * (FIRST[par] + HALF * (STEPS - 1)))
                    two_halves(dve, first, second)
                    update(NPC - 1, 1, HALF - 1)
                    evacuate(NPC - 2, 0, HALF - 1)
                    evacuate(NPC - 1, 1, HALF - 1)

                steps(dve, step)


def normalise(nc, st, h, o, a, scale, shift):
    st.mark(nc.vector.scalar_tensor_tensor(o, h[:], a[:, 0:1], o, ALU.mult, ALU.add))
    st.wait()
    st.mark(nc.vector.tensor_tensor(o, o, scale, ALU.mult))
    st.wait()
    st.mark(nc.vector.tensor_tensor(o, o, shift, ALU.add))
    st.wait()
    st.mark(nc.vector.tensor_tensor(o, o, h[:], ALU.add))


_CONV = ["W", "b", "cw", "cb", "a", "g", "be", "blank"]
_GRU = ["W_msg", "b_msg", "W_ih", "W_hh", "b_ih", "b_hh"]


def kernel(**inputs):
    import numpy as _np
    import concourse.bacc as _bacc
    from concourse import mybir as _mybir
    from concourse.bass_utils import run_bass_kernel_spmd as _run

    nc = _bacc.Bacc("TRN2", target_bir_lowering=False, num_devices=1)
    arrays = {}

    def given(name, transposed=False):
        a = _np.asarray(inputs[name])
        a = _np.ascontiguousarray(a.T if transposed else a)
        arrays[f"in_{name}_dram"] = a
        return nc.dram_tensor(f"in_{name}_dram", a.shape, _mybir.dt.from_np(a.dtype), kind="ExternalInput").ap()

    x, src, dst = given("x"), given("src"), given("dst")
    conv = [[given(f"L0_gnn_{p}{i}", p == "W") for p in _CONV] for i in range(2)]
    gru = [given(f"L1_gnn_{p}", p.startswith("W_")) for p in _GRU]
    out = nc.dram_tensor("out_0_dram", (N, D), F32, kind="ExternalOutput").ap()
    build(nc, x, src, dst, conv, gru, out)
    r = _run(nc, [arrays], core_ids=[0])
    return r.results[0]["out_0_dram"]
```
